# Optimizing a Trainium2 kernel written in Bass

```python
import numpy as np
import jax
import jax.numpy as jnp

def _softmax(x, axis=-1):
    return jax.nn.softmax(x, axis=axis)
def _gelu(x):
    return jax.nn.gelu(x, approximate=True)
def _silu(x):
    return jax.nn.silu(x)
def _sigmoid(x):
    return jax.nn.sigmoid(x)
def _layernorm(x, axis=-1, eps=1e-5):
    m = jnp.mean(x, axis=axis, keepdims=True)
    v = jnp.var(x, axis=axis, keepdims=True)
    return (x - m) / jnp.sqrt(v + eps)
def _scatter_add(tgt, idx, src, axis=0):
    return tgt.at[idx].add(src)
def _segment_sum(src, seg, n):
    return jax.ops.segment_sum(src, seg, n)

kernel_name = 'mk_vit_tower_cls_d1_tok_img256_3e24b0'

def setup_inputs(seed: int = 0):
    np.random.seed(seed)
    _w = jnp.asarray
    def _rec_inputs():
        import jax
        import jax.numpy as jnp
        _rk = jax.random.key(seed)
        x = (-0.000125008 + 0.999885 * jax.random.normal(jax.random.fold_in(_rk, 1), (32, 256, 64, 64), jnp.float32))
        cls_tok = 0.02 * jax.random.normal(jax.random.fold_in(_rk, 5), (1, 1, 256), jnp.float32)
        return x, cls_tok
    x, cls_tok = _rec_inputs()
    def _L0_tok_setup():
        import jax, jax.numpy as jnp
        import numpy as np
        B, C, H, W = (32, 256, 64, 64)
        STRIDE, HEADS = (4, 8)

        def _ln(x, w, b):
            mu = x.mean(-1, keepdims=True)
            var = ((x - mu) ** 2).mean(-1, keepdims=True)
            return (x - mu) * jax.lax.rsqrt(var + 1e-05) * w + b
        key = jax.random.key(seed)
        ks = jax.random.split(key, 4)
        return {'features': jax.random.normal(ks[0], (B, C, H, W), dtype=jnp.float32), 'ln_q_w': jnp.ones((C,), jnp.float32), 'ln_q_b': jnp.zeros((C,), jnp.float32), 'Wq': jax.random.normal(ks[1], (C, C), dtype=jnp.float32) * 0.02, 'ln_kv_w': jnp.ones((C,), jnp.float32), 'ln_kv_b': jnp.zeros((C,), jnp.float32), 'Wkv': jax.random.normal(ks[2], (2 * C, C), dtype=jnp.float32) * 0.02, 'proj_w': jax.random.normal(ks[3], (C, C), dtype=jnp.float32) * 0.02, 'proj_b': jnp.zeros((C,), jnp.float32), 'conv_stride': STRIDE, 'num_heads': HEADS}
    _L0_tok_all = _L0_tok_setup()
    _L0_tok_in = {k: v for k, v in _L0_tok_all.items() if k in ('ln_q_w', 'ln_q_b', 'Wq', 'ln_kv_w', 'ln_kv_b', 'Wkv', 'proj_w', 'proj_b', )}
    del _L0_tok_all

    def _L0_attn_setup():
        import jax, jax.numpy as jnp
        import numpy as np
        SEQ, BATCH, IN, HID = (2048, 64, 256, 256)
        key = jax.random.key(seed)
        k1, k2, k3, k4, k5 = jax.random.split(key, 5)
        s = 1.0 / np.sqrt(HID)
        return {'x_in': jax.random.normal(k1, (SEQ, BATCH, IN), dtype=jnp.float32), 'W_ih': jax.random.uniform(k2, (HID, IN), jnp.float32, -s, s), 'W_hh': jax.random.uniform(k3, (HID, HID), jnp.float32, -s, s), 'b_ih': jax.random.uniform(k4, (HID,), jnp.float32, -s, s), 'b_hh': jax.random.uniform(k5, (HID,), jnp.float32, -s, s)}
    _L0_attn_all = _L0_attn_setup()
    _L0_attn_in = {k: v for k, v in _L0_attn_all.items() if k in ('W_ih', 'W_hh', 'b_ih', 'b_hh', )}
    del _L0_attn_all

    def _L0_ffn_setup():
        import jax, jax.numpy as jnp
        import numpy as np
        NUM_EXPERTS = 8
        TOP_K = 2
        B, S, D = (8, 8192, 256)

        def _moe(tokens, router_w, w1, b1, w2, b2):
            N = tokens.shape[0]
            E = router_w.shape[0]
            logits = tokens.astype(jnp.float32) @ router_w.astype(jnp.float32).T
            probs = jax.nn.softmax(logits, axis=-1)
            rw, re = jax.lax.top_k(probs, TOP_K)
            if TOP_K > 1:
                rw = rw / jnp.maximum(rw.sum(-1, keepdims=True), 1e-12)
            rw = rw.astype(tokens.dtype)
            combine = jnp.zeros((N, E), tokens.dtype).at[jnp.arange(N)[:, None], re].set(rw)
            out = tokens
            for e in range(E):
                h = jax.nn.gelu(tokens @ w1[e] + b1[e], approximate=False)
                y = h @ w2[e] + b2[e]
                out = out + combine[:, e:e + 1] * y
            return out
        key = jax.random.key(seed)
        ks = jax.random.split(key, 4)
        scale = 1.0 / np.sqrt(D).astype(np.float32)
        return {'input_embeddings': jax.random.normal(ks[0], (B, S, D), jnp.float32), 'router_w': jax.random.normal(ks[1], (NUM_EXPERTS, D), jnp.float32) * scale, 'w1': jax.random.normal(ks[2], (NUM_EXPERTS, D, D), jnp.float32) * scale, 'b1': jnp.zeros((NUM_EXPERTS, D), jnp.float32), 'w2': jax.random.normal(ks[3], (NUM_EXPERTS, D, D), jnp.float32) * scale, 'b2': jnp.zeros((NUM_EXPERTS, D), jnp.float32)}
    _L0_ffn_all = _L0_ffn_setup()
    _L0_ffn_in = {k: v for k, v in _L0_ffn_all.items() if k in ('router_w', 'w1', 'b1', 'w2', 'b2', )}
    del _L0_ffn_all

    return {
        "x": x,
        "cls_tok": cls_tok,
        "L0_tok_ln_q_w": _L0_tok_in["ln_q_w"],
        "L0_tok_ln_q_b": _L0_tok_in["ln_q_b"],
        "L0_tok_Wq": _L0_tok_in["Wq"],
        "L0_tok_ln_kv_w": _L0_tok_in["ln_kv_w"],
        "L0_tok_ln_kv_b": _L0_tok_in["ln_kv_b"],
        "L0_tok_Wkv": _L0_tok_in["Wkv"],
        "L0_tok_proj_w": _L0_tok_in["proj_w"],
        "L0_tok_proj_b": _L0_tok_in["proj_b"],
        "L0_attn_W_ih": _L0_attn_in["W_ih"],
        "L0_attn_W_hh": _L0_attn_in["W_hh"],
        "L0_attn_b_ih": _L0_attn_in["b_ih"],
        "L0_attn_b_hh": _L0_attn_in["b_hh"],
        "L0_ffn_router_w": _L0_ffn_in["router_w"],
        "L0_ffn_w1": _L0_ffn_in["w1"],
        "L0_ffn_b1": _L0_ffn_in["b1"],
        "L0_ffn_w2": _L0_ffn_in["w2"],
        "L0_ffn_b2": _L0_ffn_in["b2"],
    }

def reference(x, cls_tok, L0_tok_ln_q_w, L0_tok_ln_q_b, L0_tok_Wq, L0_tok_ln_kv_w, L0_tok_ln_kv_b, L0_tok_Wkv, L0_tok_proj_w, L0_tok_proj_b, L0_attn_W_ih, L0_attn_W_hh, L0_attn_b_ih, L0_attn_b_hh, L0_ffn_router_w, L0_ffn_w1, L0_ffn_b1, L0_ffn_w2, L0_ffn_b2):
    import jax
    import jax.numpy as jnp
    def _L0_tok_ref(features, ln_q_w, ln_q_b, Wq, ln_kv_w, ln_kv_b, Wkv, proj_w, proj_b, conv_stride, num_heads):
        import jax, jax.numpy as jnp
        import numpy as np
        B, C, H, W = (32, 256, 64, 64)
        STRIDE, HEADS = (4, 8)

        def _ln(x, w, b):
            mu = x.mean(-1, keepdims=True)
            var = ((x - mu) ** 2).mean(-1, keepdims=True)
            return (x - mu) * jax.lax.rsqrt(var + 1e-05) * w + b
        s = conv_stride
        b, c, hh, ww = features.shape
        h, w = (hh // s, ww // s)
        hw, n, d = (h * w, s * s, c // num_heads)
        scale = c ** (-0.5)
        x = features.reshape(b, c, h, s, w, s)
        reduce_feats = x.mean((3, 5)).reshape(b, c, hw).transpose(0, 2, 1)
        unf = x.transpose(0, 1, 2, 4, 3, 5).reshape(b, c, hw, n).transpose(0, 2, 3, 1)
        q = _ln(reduce_feats, ln_q_w, ln_q_b) @ Wq.T
        q = q.reshape(b, hw, num_heads, d).transpose(0, 2, 1, 3)
        kv = _ln(unf, ln_kv_w, ln_kv_b) @ Wkv.T
        kv = kv.reshape(b, hw, n, 2, num_heads, d).transpose(3, 0, 4, 1, 2, 5)
        k, v = (kv[0], kv[1])
        attn = jax.nn.softmax(jnp.einsum('bhpd,bhpnd->bhpn', q * scale, k), axis=-1)
        aggre = jnp.einsum('bhpn,bhpnd->bhpd', attn, v)
        aggre = aggre.transpose(0, 2, 1, 3).reshape(b, hw, c)
        return reduce_feats + aggre @ proj_w.T + proj_b

    def _L0_attn_ref(x_in, W_ih, W_hh, b_ih, b_hh):
        import jax, jax.numpy as jnp
        import numpy as np
        SEQ, BATCH, IN, HID = (2048, 64, 256, 256)
        xp = jnp.einsum('tbi,hi->tbh', x_in, W_ih) + b_ih + b_hh
        h0 = jnp.zeros((x_in.shape[1], W_hh.shape[0]), dtype=x_in.dtype)

        def step(h, xp_t):
            h_new = jnp.tanh(xp_t + h @ W_hh.T)
            return (h_new, h_new)
        _, hiddens = jax.lax.scan(step, h0, xp)
        return hiddens

    def _L0_ffn_ref(input_embeddings, router_w, w1, b1, w2, b2):
        import jax, jax.numpy as jnp
        import numpy as np
        NUM_EXPERTS = 8
        TOP_K = 2
        B, S, D = (8, 8192, 256)

        def _moe(tokens, router_w, w1, b1, w2, b2):
            N = tokens.shape[0]
            E = router_w.shape[0]
            logits = tokens.astype(jnp.float32) @ router_w.astype(jnp.float32).T
            probs = jax.nn.softmax(logits, axis=-1)
            rw, re = jax.lax.top_k(probs, TOP_K)
            if TOP_K > 1:
                rw = rw / jnp.maximum(rw.sum(-1, keepdims=True), 1e-12)
            rw = rw.astype(tokens.dtype)
            combine = jnp.zeros((N, E), tokens.dtype).at[jnp.arange(N)[:, None], re].set(rw)
            out = tokens
            for e in range(E):
                h = jax.nn.gelu(tokens @ w1[e] + b1[e], approximate=False)
                y = h @ w2[e] + b2[e]
                out = out + combine[:, e:e + 1] * y
            return out
        b, s, d = input_embeddings.shape
        tokens = input_embeddings.reshape(b * s, d)
        return _moe(tokens, router_w, w1, b1, w2, b2).reshape(b, s, d)

    h = _L0_tok_ref(x, L0_tok_ln_q_w, L0_tok_ln_q_b, L0_tok_Wq, L0_tok_ln_kv_w, L0_tok_ln_kv_b, L0_tok_Wkv, L0_tok_proj_w, L0_tok_proj_b, 4, 8)
    h = jnp.concatenate([jnp.broadcast_to(cls_tok, (h.shape[0], 1, h.shape[2])), h], axis=1)
    h = h + _L0_attn_ref(_layernorm(h, axis=-1), L0_attn_W_ih, L0_attn_W_hh, L0_attn_b_ih, L0_attn_b_hh)
    h = h + _L0_ffn_ref(_layernorm(h, axis=-1), L0_ffn_router_w, L0_ffn_w1, L0_ffn_b1, L0_ffn_w2, L0_ffn_b2)
    return h


_drawn_inputs = setup_inputs


def setup_inputs(seed=0):
    import zlib

    import numpy as np

    out = dict(_drawn_inputs(seed))
    spreads = {'L0_tok_ln_q_w': (1.0, 0.6),
     'L0_tok_ln_q_b': (0.0, 2.0),
     'L0_tok_ln_kv_w': (1.0, 0.2),
     'L0_tok_ln_kv_b': (0.0, 0.1),
     'L0_tok_proj_b': (0.0, 0.1),
     'L0_ffn_b1': (0.0, 0.1),
     'L0_ffn_b2': (0.0, 0.1)}
    factors = {'L0_tok_Wq': 3.915}
    for name, (base, spread) in spreads.items():
        noise = np.random.default_rng([zlib.crc32(name.encode()), seed]).standard_normal(out[name].shape)
        drawn = base * np.exp(spread * noise) if base else spread * noise
        out[name] = jnp.asarray(drawn.astype(out[name].dtype))
    for name, factor in factors.items():
        out[name] = (out[name] * factor).astype(out[name].dtype)
    return out
```

```python
from contextlib import ExitStack

import concourse.bass as bass
from concourse import mybir

P = 128
F32 = mybir.dt.float32
F16 = mybir.dt.float16
ALU = mybir.AluOpType
ACT = mybir.ActivationFunctionType
X = mybir.AxisListType.X

B, C, IMG, STRIDE = 32, 256, 64, 4
HEADS, E = 8, 8
NPIX = STRIDE * STRIDE
D = C // HEADS
CC = C // P
TOKS = (IMG // STRIDE) ** 2
UNITS = B * TOKS // P
HALVES = TOKS // P
GP = P // NPIX
G = P // GP
PIX = P * NPIX
XBUF = 4
PT = 64
WSC = 64.0
EPS = 1e-5
TPC = 4
CHUNKS = UNITS // TPC


class Turn:

    width = 1

    def __init__(self, j, k):
        self.j, self.k = j, k
        self.two = k % 2

    def count(self, per, plus):
        return self.j * (self.width * per) + (self.k * per + plus)


class Unit(Turn):

    width = XBUF

    def __init__(self, j, k):
        super().__init__(j, k)
        self.x = k % XBUF

    def before(self, n=1):
        return Unit(self.j, self.k - n)


class Chunk(Turn):

    width = 2

    def __init__(self, j, k, last=False):
        super().__init__(j, k)
        self.last = last
        self.tiles = 1 if last else TPC
        self.rows = B if last else P
        self.cols = self.tiles * self.rows
        self.fills = (self.tiles + 1) // 2

    def next(self):
        return Chunk(self.j, self.k + 1, isinstance(self.j, int) and self.j * 2 + self.k + 1 == CHUNKS)


def wait(eng, sem, unit, per, plus):
    v = unit.count(per, plus)
    if isinstance(v, int) and v <= 0:
        return
    eng.wait_ge(sem, v)


def wait_all(eng, waits):
    values = [(sem, unit.count(per, plus)) for sem, unit, per, plus in waits]
    for _, v in values:
        eng.compute_val(v)
    for sem, v in values:
        if not isinstance(v, int) or v > 0:
            eng.wait_ge(sem, v)


def over_slots(eng, slot, spare=0):
    last = UNITS // XBUF - 1
    for k in range(3):
        slot(eng, Unit(0, k), True, k >= 1, k >= 2)
    with eng.Fori(0, last - spare) as j:
        for k in range(3, XBUF + 3):
            slot(eng, Unit(j, k), True, True, True)
    for n in range(spare):
        for k in range(3, XBUF + 3):
            slot(eng, Unit(last - spare + n, k), True, True, True)
    slot(eng, Unit(last, 3), True, True, True)
    slot(eng, Unit(last, 4), False, True, True)
    slot(eng, Unit(last, 5), False, False, True)


def vit_tower(nc, xg, cls_tok, ln_q_w, ln_q_b, wqT, ln_kv_w, ln_kv_w_col, ln_kv_b, wk, wvT, projT, proj_b,
              wihT, whhT, b_ih, b_hh, routerT, w1, b1, w2, b2, ident_in, mask_in, iota_in, out):
    h2_dram = nc.dram_tensor("h2_dram", [UNITS, P, C], F32, kind="Internal").ap()
    ctx = ExitStack()
    with ctx:
        def sb(name, shape, dt=F32):
            return ctx.enter_context(nc.sbuf_tensor(name, shape, dt))

        def sem(name):
            return ctx.enter_context(nc.semaphore(name))

        ident = sb("ident", [P, P])
        ident16 = sb("ident16", [P, P], F16)
        mask16 = sb("mask16", [P, GP], F16)
        mask = sb("mask", [P, GP])
        avg = sb("avg", [P, P])
        lq_w = sb("lq_w", [P, CC])
        lq_b = sb("lq_b", [P, CC])
        lkv_w = sb("lkv_w", [P, CC])
        lkv_b = sb("lkv_b", [P, CC])
        bih_c = sb("bih_c", [P, CC])
        bhh_c = sb("bhh_c", [P, CC])
        rnn_b = sb("rnn_b", [P, CC])
        cls_row = sb("cls_row", [B, C])
        wq_s = sb("wq_s", [P, CC, C])
        wvh = sb("wvh", [P, CC, C], F16)
        wvl = sb("wvl", [P, CC, C], F16)
        pj_s = sb("pj_s", [P, CC, C])
        ih_s = sb("ih_s", [P, CC, C])
        hh_s = sb("hh_s", [P, CC, C])
        qb_row = sb("qb_row", [P, C])
        cvec = sb("cvec", [P, C])
        wk_st = sb("wk_st", [P, HEADS, C], F16)
        eps_c = sb("eps_c", [P, 1])
        held = sb("held", [P, 1])
        half_neg = sb("half_neg", [P, G])
        b1_s = sb("b1_s", [P, E, CC])
        clsH = sb("clsH", [P, CC, B])

        stage_a = ExitStack()
        def sa(name, shape, dt=F32):
            return stage_a.enter_context(nc.sbuf_tensor(name, shape, dt))
        x_s = [sa(f"x{i}", [P, CC, PIX]) for i in range(XBUF)]
        xTh = [sa(f"xTh{i}", [P, G, C], F16) for i in range(XBUF)]
        xTl = [sa(f"xTl{i}", [P, G, C], F16) for i in range(XBUF)]
        r_s = [sa(f"r{i}", [P, CC, P]) for i in range(2)]
        rT = sa("rT", [P, C])
        rc = [sa(f"rc{i}", [P, C]) for i in range(XBUF)]
        add8 = sa("add8", [P, PT, 8])
        add4 = sa("add4", [P, PT, 4])
        add2 = sa("add2", [P, PT, 2])
        q_s = sa("q_s", [P, C])
        qs = sa("qs", [P, HEADS, 4, D], F16)
        qsT = sa("qsT", [P, HEADS, P], F16)
        u_s = [sa(f"u{i}", [P, CC, HEADS, P]) for i in range(2)]
        zh = sa("zh", [P, CC, HEADS, P], F16)
        zl = sa("zl", [P, CC, HEADS, P], F16)
        sm = sa("sm", [P, G // 2 * HEADS, GP])
        sc = sa("sc", [P, G, HEADS])
        sc2 = sa("sc2", [P, G, HEADS])
        mx = sa("mx", [P, GP])
        lg = sa("lg", [P, GP, NPIX])
        ex = sa("ex", [P, GP, NPIX])
        den = sa("den", [P, GP])
        rden = sa("rden", [P, GP])
        pr = sa("pr", [P, GP, NPIX])
        pc = sa("pc", [P, G, HEADS])
        pch = sa("pch", [P, G, HEADS], F16)
        pcl = sa("pcl", [P, G, HEADS], F16)
        pdh = sa("pdh", [P, G, HEADS, GP], F16)
        pdl = sa("pdl", [P, G, HEADS, GP], F16)
        st = sa("st", [P, G, 6])
        v_a = sa("v_a", [P, G])
        v_b = sa("v_b", [P, G])
        v_c = sa("v_c", [P, G])
        v_d = sa("v_d", [P, G])
        v_e = sa("v_e", [P, G])
        rs_px = [sa(f"rs_px{i}", [P, G]) for i in range(2)]
        qst = sa("qst", [P, 6])
        qmv = sa("qmv", [P, 2])
        qve = sa("qve", [P, 1])
        q_rs = sa("q_rs", [P, 1])
        ag = sa("ag", [P, C])
        agT = sa("agT", [P, CC, P])
        h_s = [sa(f"h{i}", [P, C]) for i in range(2)]
        hst = sa("hst", [P, 6])
        hmv = sa("hmv", [P, 2])
        hve = sa("hve", [P, 1])
        h_rs = sa("h_rs", [P, 1])
        xn = sa("xn", [P, C])
        xnT = sa("xnT", [P, CC, P + 1])
        hT = [sa(f"hT{i}", [P, CC, P + 1]) for i in range(2)]
        h2 = sa("h2", [P, C])

        pbank = [ctx.enter_context(nc.psum_tensor(f"bank{i}", [P, 512], F32)) for i in range(8)]
        TX, US, ZB, MI = pbank[0:2], pbank[2:4], pbank[4:6], pbank[6:8]
        UB = [US[1], ZB[0], ZB[1], US[1]]

        names = """consts_in wk_in cls_in prep_in x0_in x1_in x2_in x3_in
            avg_set prep_pe prep_act prep_dve prep_pool cls_pe cls_dve cls_act cls_pool w_ready_dve w_ready_act
            pool_adds r_done qve_done q_rs_done rc_done px_ve_done rs_px_done h_rs_done pd_done clsH_done hve_done
            z_low pc_split tx_free
            rT_ps q_ps qs_ps u_ps xT_ps s_ps c_ps pt_ps z_ps a_ps at_ps pj_ps nt_ps h_ps ht_ps
            rT_done xT_done u_done z_done ag_done agT_done ex_done xnT_done hT_done
            q_stat q_var q_done q_split qsT_done st_done px_var s_masked s_summed sc_done c_max c_sub
            p_sum p_rec p_done pc_done h_done h_stat h_var xn_done h2_done h2_out""".split()
        s = {n: sem(n) for n in names}
        x_in = [s["x0_in"], s["x1_in"], s["x2_in"], s["x3_in"]]

        stage_wk = x_s[1][:, :, :].rearrange("p c (h n) -> p (c h) n", n=C)[:, 0:HEADS, :]
        stage_wk32 = x_s[1][:, :, :].rearrange("p c (h n) -> p (c h) n", n=C)[:, HEADS:2 * HEADS, :]
        stage = x_s[2][:, :, :].rearrange("p c (h n) -> p (c h) n", n=C)
        raw_q, raw_v, sq, sv, cv32 = [stage[:, n * CC:(n + 1) * CC, :] for n in range(5)]
        bq_rep = stage[:, 10, :].rearrange("p (c n) -> p c n", n=P)
        vb_rep = stage[:, 11, :].rearrange("p (c n) -> p c n", n=P)
        vb_col, wk_sum, wk_mean = stage[:, 12, 0:CC], stage[:, 12, 8:8 + HEADS], stage[:, 12, 16:16 + HEADS]
        cst, cmv, cve, crs = [stage[0:B, 13, a:b] for a, b in ((0, 6), (8, 10), (12, 13), (16, 17))]
        cxn = stage[0:B, 14, :]
        lkv_w_row = stage[:, 15, :]
        projb_row = u_s[1][:, 0, 0:C // P, :].rearrange("p a n -> p (a n)")

        NCONST = 17
        tokens = ExitStack()
        block = tokens.enter_context(nc.Block())

        def sync_prep(sp):
            row = lambda a, n: a.partition_broadcast(n)
            loads = [(ident[:, :], ident_in), (mask[:, :], mask_in),
                     (lq_w[:, :], ln_q_w), (lq_b[:, :], ln_q_b),
                     (lkv_w[:, :], ln_kv_w_col), (lkv_b[:, :], ln_kv_b),
                     (bih_c[:, :], b_ih), (bhh_c[:, :], b_hh),
                     (projb_row[:, :], row(proj_b, P)), (lkv_w_row[:, :], row(ln_kv_w, P)),
                     (cls_row[:, :], row(cls_tok, B)),
                     (raw_q, wqT.rearrange("(c p) n -> p c n", p=P)),
                     (raw_v, wvT.rearrange("(c p) n -> p c n", p=P)),
                     (pj_s[:, :, :], projT.rearrange("(c p) n -> p c n", p=P)),
                     (ih_s[:, :, :], wihT.rearrange("(c p) n -> p c n", p=P)),
                     (hh_s[:, :, :], whhT.rearrange("(c p) n -> p c n", p=P)),
                     (b1_s[:, :, :], b1.rearrange("p (e c) -> p e c", e=E))]
            assert len(loads) == NCONST
            for dst, src in loads:
                sp.dma_start(dst, src).then_inc(s["consts_in"], 16)
            for rep in range(4):
                sp.dma_start(stage_wk[rep * D:(rep + 1) * D, :, :],
                             wk.rearrange("(h d) n -> d h n", d=D)).then_inc(s["wk_in"], 16)

        def load_x(sp, u, ahead):
            n = u.j * XBUF + (u.k + ahead)
            n = n if isinstance(n, int) else sp.snap(n, min_val=0, max_val=UNITS - 1)
            t = Unit(u.j, u.k + ahead - XBUF)
            if not (isinstance(t.j, int) and t.j * XBUF + t.k < 0):
                wait_all(sp, [(s["xT_ps"], t, 8, 8), (s["s_ps"], t, 2, 2), (s["r_done"], t, 1, 1)])
            k = (u.k + ahead) % XBUF
            sp.dma_start(x_s[k][:, :, :], xg[n]).then_inc(x_in[k], 16)

        def wait_x(eng, u):
            eng.wait_ge(x_in[u.x], u.j * 16 + (u.k // XBUF + 1) * 16)

        @block.sync
        def _(sp):
            sp.dma_start(x_s[0][:, :, :], xg[0]).then_inc(x_in[0], 16)
            sync_prep(sp)
            sp.dma_start(x_s[3][:, :, :], xg[3]).then_inc(x_in[3], 16)
            sp.wait_ge(s["w_ready_dve"], 1)
            sp.wait_ge(s["w_ready_act"], 1)
            for n in (1, 2):
                sp.dma_start(x_s[n][:, :, :], xg[n]).then_inc(x_in[n], 16)

            def slot(sp, u, front, mid, back):
                v, w = u.before(), u.before(2)
                if mid:
                    t = v.j * XBUF + v.k
                    if not isinstance(t, int) or t + XBUF < UNITS:
                        load_x(sp, v, XBUF)
                if back:
                    n = w.j * XBUF + w.k
                    n = n if isinstance(n, int) else sp.snap(n, min_val=0, max_val=UNITS - 1)
                    wait_all(sp, [(s["h2_done"], w, 1, 1)])
                    sp.dma_start(h2_dram[n], h2[:, :]).then_inc(s["h2_out"], 16)
            over_slots(sp, slot, 1)
            sp.wait_ge(s["h2_out"], 16 * UNITS)

        @block.gpsimd
        def _(pool):
            pool.memset(avg[:, :], 1.0 / C).then_inc(s["avg_set"], 1)
            pool.memset(half_neg[:, :], -0.5).then_inc(s["avg_set"], 1)
            pool.memset(eps_c[:, :], EPS).then_inc(s["avg_set"], 1)
            for i in range(2):
                pool.memset(hT[i][:, :, :], 0.0).then_inc(s["avg_set"], 1)
            pool.memset(xnT[:, :, :], 0.0).then_inc(s["avg_set"], 1)
            pool.wait_ge(s["avg_set"], 6)
            pool.wait_ge(s["cls_dve"], 3)
            pool.tensor_tensor(crs, cve, half_neg[0:B, 0:1], ALU.pow).then_inc(s["cls_pool"], 1)

            STEPS = CC * P // PT

            def pooling(pool, u, c, q, q0):
                xv = x_s[u.x][:, c, :].rearrange("p (t n) -> p t n", n=NPIX)[:, q * PT:(q + 1) * PT, :]
                base = 3 * q0
                pool.tensor_tensor(add8[:, :, :], xv[:, :, 0:8], xv[:, :, 8:16], ALU.add).then_inc(s["pool_adds"], 1)
                wait(pool, s["pool_adds"], u, 3 * STEPS, base + 1)
                pool.tensor_tensor(add4[:, :, :], add8[:, :, 0:4], add8[:, :, 4:8], ALU.add).then_inc(s["pool_adds"], 1)
                wait(pool, s["pool_adds"], u, 3 * STEPS, base + 2)
                pool.tensor_tensor(add2[:, :, :], add4[:, :, 0:2], add4[:, :, 2:4], ALU.add).then_inc(s["pool_adds"], 1)
                wait(pool, s["pool_adds"], u, 3 * STEPS, base + 3)
                i = pool.tensor_tensor(r_s[u.two][:, c, q * PT:(q + 1) * PT], add2[:, :, 0], add2[:, :, 1], ALU.add)
                if q0 == STEPS - 1:
                    i.then_inc(s["r_done"], 1)

            def pool_part(pool, u, parts):
                for n in parts:
                    if n == 0:
                        wait_x(pool, u)
                        wait(pool, s["q_ps"], u, 1, -1)
                    pooling(pool, u, n // (P // PT), n % (P // PT), n)

            pool_part(pool, Unit(0, 0), range(STEPS))

            def slot(pool, u, front, mid, back):
                v, w = u.before(), u.before(2)
                nxt = Unit(u.j, u.k + 1)
                more = front and not (isinstance(u.j, int) and u.j * XBUF + u.k + 1 >= UNITS)
                if front:
                    wait(pool, s["q_var"], u, 1, 1)
                    pool.tensor_tensor(qve[:, :], qmv[:, 1:2], eps_c[:, :], ALU.add).then_inc(s["qve_done"], 1)
                    wait(pool, s["qve_done"], u, 1, 1)
                    pool.tensor_tensor(q_rs[:, :], qve[:, :], half_neg[:, 0:1], ALU.pow).then_inc(s["q_rs_done"], 1)
                if back:
                    wait(pool, s["pc_split"], w, 2, 2)
                    for part, dst in ((pch, pdh), (pcl, pdl)):
                        pool.tensor_tensor(dst[:, :, :, :].rearrange("p g h t -> p (g h) t"),
                                           part[:, :, :].rearrange("p g h -> p (g h)").unsqueeze(2).to_broadcast([P, G * HEADS, GP]),
                                           mask16[:, :].unsqueeze(1).to_broadcast([P, G * HEADS, GP]),
                                           ALU.mult).then_inc(s["pd_done"], 1)
                if mid:
                    wait(pool, s["px_var"], v, 3, 3)
                    pool.tensor_tensor(rs_px[v.two][:, :], v_e[:, :], half_neg[:, :], ALU.pow).then_inc(s["rs_px_done"], 1)
                if front:
                    wait(pool, s["rT_done"], u, 1, 1)
                    if isinstance(u.j, int) and u.j * XBUF + u.k == 0:
                        pool.wait_ge(s["w_ready_dve"], 1)
                    wait(pool, s["h_done"], u, 1, -2)
                    pool.tensor_tensor(rc[u.x][:, :], rT[:, :], cvec[:, :], ALU.add).then_inc(s["rc_done"], 1)
                if more:
                    pool_part(pool, nxt, range(0, STEPS // 2))
                if back:
                    wait(pool, s["h_var"], w, 1, 1)
                    pool.tensor_tensor(hve[:, :], hmv[:, 1:2], eps_c[:, :], ALU.add).then_inc(s["hve_done"], 1)
                    wait(pool, s["hve_done"], w, 1, 1)
                    pool.tensor_tensor(h_rs[:, :], hve[:, :], half_neg[:, 0:1], ALU.pow).then_inc(s["h_rs_done"], 1)
                if more:
                    pool_part(pool, nxt, range(STEPS // 2, STEPS))
                if back and w.two == 0:
                    wait(pool, s["hT_done"], w, 2, 2)
                    b = w.j * HALVES + w.k // HALVES
                    pool.tensor_copy(clsH[:, :, bass.ds(b, 1)], hT[0][:, :, P:P + 1]).then_inc(s["clsH_done"], 1)
            over_slots(pool, slot)

        @block.scalar
        def _(act):
            act.wait_ge(s["consts_in"], 16 * NCONST)
            act.wait_ge(s["avg_set"], 6)
            act.activation(rnn_b[:, 0:1], bih_c[:, 0:1], ACT.Identity, bias=bhh_c[:, 0:1]).then_inc(s["prep_act"], 1)
            act.activation(rnn_b[:, 1:2], bih_c[:, 1:2], ACT.Identity, bias=bhh_c[:, 1:2]).then_inc(s["prep_act"], 1)
            act.wait_ge(s["prep_pe"], 3)
            act.activation(vb_col, MI[0][:, 0:CC], ACT.Copy).then_inc(s["prep_act"], 1)
            act.wait_ge(s["cls_pe"], 1)
            act.activation(xnT[:, :, P:P + 1], MI[1][:, 0:CC * B].rearrange("p (c b) -> p c b", b=B)[:, :, 0:1],
                           ACT.Copy).then_inc(s["w_ready_act"], 1)

            def x_out(act, u, fills):
                for f in fills:
                    wait(act, s["xT_ps"], u, 8, f + 1)
                    act.activation(xTh[u.x][:, 2 * f:2 * f + 2, :],
                                   TX[f % 2][:, :].rearrange("p (g c) -> p g c", c=C), ACT.Copy).then_inc(s["xT_done"], 1)

            def z_out(act, w, fills):
                for f in fills:
                    wait(act, s["z_ps"], w, 4, f + 1)
                    c, half = f // 2, f % 2
                    act.activation(zh[:, c, :, half * 64:half * 64 + 64], ZB[f % 2][:, :].rearrange("p (h n) -> p h n", n=64),
                                   ACT.Copy, scale=1.0 / WSC).then_inc(s["z_done"], 1)

            def slot(act, u, front, mid, back):
                v, w = u.before(), u.before(2)
                if front:
                    wait(act, s["rT_ps"], u, 1, 1)
                    wait(act, s["rc_done"], u, 1, 0)
                    act.activation(rT[:, :], MI[1][:, 0:C], ACT.Copy, scale=1.0 / NPIX).then_inc(s["rT_done"], 1)
                    x_out(act, u, [0, 1, 2])
                if back:
                    z_out(act, w, [0, 1])
                if front:
                    wait(act, s["qs_ps"], u, 1, 1)
                    act.activation(qsT[:, :, :].rearrange("p h t -> p (h t)"), MI[1][:, :].bitcast(F16),
                                   ACT.Copy).then_inc(s["qsT_done"], 1)
                    x_out(act, u, [3])
                if back:
                    z_out(act, w, [2, 3])
                    wait(act, s["a_ps"], w, 1, 1)
                    act.activation(ag[:, :], MI[0][:, 0:C], ACT.Copy, scale=1.0 / WSC).then_inc(s["ag_done"], 1)
                if front:
                    x_out(act, u, [4])
                    for f in range(4):
                        wait(act, s["u_ps"], u, 4, f + 1)
                        c, hh = f // 2, f % 2
                        act.activation(u_s[u.two][:, c, hh * 4:hh * 4 + 4, :].rearrange("p h t -> p (h t)"),
                                       UB[f][:, :], ACT.Copy, scale=C ** -0.5 / WSC).then_inc(s["u_done"], 1)
                if back:
                    wait(act, s["at_ps"], w, 1, 1)
                    act.activation(agT[:, :, :].rearrange("p c t -> p (c t)"), MI[1][:, 0:C], ACT.Copy).then_inc(s["agT_done"], 1)
                if front:
                    x_out(act, u, [5, 6])
                if back:
                    wait(act, s["nt_ps"], w, 1, 1)
                    act.activation(xnT[:, :, 0:P], MI[1][:, 0:C].rearrange("p (c t) -> p c t", t=P),
                                   ACT.Copy).then_inc(s["xnT_done"], 1)
                    wait(act, s["h_ps"], w, 1, 1)
                    n = P + 1 if w.two == 0 else P
                    if w.two == 0:
                        b = w.j * HALVES + w.k // HALVES
                        if not (isinstance(b, int) and b == 0):
                            act.wait_ge(s["clsH_done"], b)
                    for m in range(CC):
                        act.activation(hT[w.two][:, m, 0:n], MI[0][:, m * 256:m * 256 + n], ACT.Tanh,
                                       bias=rnn_b[:, m:m + 1]).then_inc(s["hT_done"], 1)
                if front:
                    x_out(act, u, [7])
                if mid:
                    wait(act, s["c_sub"], v, 1, 1)
                    act.activation(ex[:, :, :], lg[:, :, :], ACT.Exp).then_inc(s["ex_done"], 1)
            over_slots(act, slot)

        @block.tensor
        def _(pe):
            mm = pe.matmul
            pe.wait_ge(s["consts_in"], 16 * NCONST)
            pe.wait_ge(s["avg_set"], 6)
            pe.wait_ge(s["prep_dve"], 4)
            for i, w in ((0, sq), (1, sv)):
                for c in range(CC):
                    last = mm(US[i][:, 0:C], avg[:, :], w[:, c, :], start=(c == 0), stop=(c == CC - 1))
                last.then_inc(s["prep_pe"], 1)
            for m in range(CC):
                for c in range(CC):
                    last = mm(MI[0][:, m:m + 1], raw_v[:, c, m * P:(m + 1) * P], lkv_b[:, c:c + 1],
                              start=(c == 0), stop=(c == CC - 1))
            last.then_inc(s["prep_pe"], 1)
            pe.wait_ge(s["prep_dve"], 6)
            for c in range(CC):
                last = mm(ZB[0][:, 0:C], bq_rep[:, c, :], raw_q[:, c, :], start=(c == 0), stop=(c == CC - 1))
            last.then_inc(s["prep_pe"], 1)
            pe.wait_ge(s["prep_dve"], 10)
            for c in range(CC):
                last = mm(ZB[1][:, 0:C], vb_rep[:, c, :], pj_s[:, c, :], start=(c == 0), stop=(c == CC - 1))
            last.then_inc(s["prep_pe"], 1)
            pe.wait_ge(s["cls_dve"], 4)
            for c in range(CC):
                last = pe.transpose(MI[1][:, c * B:(c + 1) * B], cxn[:, c * P:(c + 1) * P], ident[0:B, 0:B])
            last.then_inc(s["cls_pe"], 1)
            pe.wait_ge(s["w_ready_dve"], 1)
            pe.wait_ge(s["w_ready_act"], 1)

            def x_turn(pe, u, fills):
                for f in fills:
                    wait(pe, s["tx_free"], u, 8, f - 1)
                    for i in range(2):
                        g = 2 * f + i
                        for c in range(CC):
                            last = pe.transpose(TX[f % 2][:, i * C + c * P:i * C + (c + 1) * P],
                                                x_s[u.x][:, c, g * P:(g + 1) * P], ident[:, :])
                    last.then_inc(s["xT_ps"], 1)

            def weigh(pe, w, fills):
                for f in fills:
                    c, half = f // 2, f % 2
                    if f == 0:
                        wait(pe, s["pd_done"], w, 2, 2)
                        wait(pe, s["tx_free"], w, 8, 8)
                    elif f == 1:
                        wait(pe, s["h2_done"], w, 1, 0)
                    else:
                        wait(pe, s["z_low"], w, 4, f - 1)
                    bank = ZB[f % 2][:, :].rearrange("p (h n) -> p h n", n=64)
                    for i in range(8):
                        g = half * 8 + i
                        o = bank[:, :, i * GP:(i + 1) * GP]
                        hi, lo = xTh[w.x][:, g, c * P:(c + 1) * P], xTl[w.x][:, g, c * P:(c + 1) * P]
                        mm(o, hi, pdh[:, g, :, :], start=True, stop=False)
                        mm(o, hi, pdl[:, g, :, :], start=False, stop=False)
                        last = mm(o, lo, pdh[:, g, :, :], start=False, stop=True)
                    last.then_inc(s["z_ps"], 1)

            def score(pe, v, quarter):
                f = quarter // 2
                if quarter == 0:
                    wait(pe, s["u_done"], v, 4, 4)
                if quarter % 2 == 0:
                    wait(pe, s["s_masked"], v, 2, f)
                for i in range(4 * (quarter % 2), 4 * (quarter % 2) + 4):
                    g = f * 8 + i
                    for c in range(CC):
                        last = mm(US[0][:, i * 64:(i + 1) * 64], x_s[v.x][:, c, g * P:(g + 1) * P],
                                  u_s[v.two][:, c, :, g * GP:(g + 1) * GP], start=(c == 0), stop=(c == CC - 1))
                if quarter % 2:
                    last.then_inc(s["s_ps"], 1)

            def project(pe, u, w, f):
                if f == 0:
                    wait(pe, s["qsT_done"], u, 1, 1)
                    wait(pe, s["u_done"], u, 4, 0)
                elif f == 3:
                    wait(pe, s["u_done"], u, 4, 1)
                else:
                    wait(pe, s["z_low"], w, 4, f + 2)
                c, hh = f // 2, f % 2
                for i in range(4):
                    h = hh * 4 + i
                    last = mm(UB[f][:, i * P:(i + 1) * P], wk_st[:, h, c * P:(c + 1) * P], qsT[:, h, :],
                              start=True, stop=True)
                last.then_inc(s["u_ps"], 1)

            def slot(pe, u, front, mid, back):
                v, w = u.before(), u.before(2)
                if front:
                    wait_x(pe, u)
                    wait(pe, s["r_done"], u, 1, 1)
                    wait(pe, s["xnT_done"], w, 1, 0)
                    for c in range(CC):
                        last = pe.transpose(MI[1][:, c * P:(c + 1) * P], r_s[u.two][:, c, :], ident[:, :])
                    last.then_inc(s["rT_ps"], 1)
                    x_turn(pe, u, [0])
                if back:
                    wait(pe, s["p_done"], w, 1, 1)
                    pe.transpose(ZB[0][:, 0:P], pr[:, :, :].rearrange("p t n -> p (t n)"), ident[:, :]).then_inc(s["pt_ps"], 1)
                if mid:
                    score(pe, v, 0)
                if front:
                    x_turn(pe, u, [1])
                    wait(pe, s["hT_done"], w, 2, 0)
                    for c in range(CC):
                        last = mm(MI[0][:, 0:C], r_s[u.two][:, c, :], wq_s[:, c, :], start=(c == 0), stop=(c == CC - 1))
                    last.then_inc(s["q_ps"], 1)
                if mid:
                    score(pe, v, 1)
                if front:
                    x_turn(pe, u, [2])
                if back:
                    weigh(pe, w, [0, 1])
                if front:
                    wait(pe, s["q_split"], u, 3, 3)
                    wait(pe, s["rT_done"], u, 1, 1)
                    q16 = MI[1][:, :].bitcast(F16)
                    for h in range(HEADS):
                        last = pe.transpose(q16[:, h * P:(h + 1) * P], qs[:, h, :, :].rearrange("p a d -> p (a d)"),
                                            ident16[:, :])
                    last.then_inc(s["qs_ps"], 1)
                    x_turn(pe, u, [3])
                if back:
                    weigh(pe, w, [2, 3])
                if mid:
                    score(pe, v, 2)
                if back:
                    wait(pe, s["z_low"], w, 4, 4)
                    if front:
                        wait(pe, s["q_done"], u, 1, 1)
                    for h in range(HEADS):
                        o = MI[0][:, h * D:(h + 1) * D]
                        for c in range(CC):
                            wh, wl = wvh[:, c, h * D:(h + 1) * D], wvl[:, c, h * D:(h + 1) * D]
                            mm(o, zh[:, c, h, :], wh, start=(c == 0), stop=False)
                            mm(o, zh[:, c, h, :], wl, start=False, stop=False)
                            last = mm(o, zl[:, c, h, :], wh, start=False, stop=(c == CC - 1))
                    last.then_inc(s["a_ps"], 1)
                if front:
                    x_turn(pe, u, [4])
                    for f in range(4):
                        project(pe, u, w, f)
                if back:
                    wait(pe, s["ag_done"], w, 1, 1)
                    if front:
                        wait(pe, s["qsT_done"], u, 1, 1)
                    for c in range(CC):
                        last = pe.transpose(MI[1][:, c * P:(c + 1) * P], ag[:, c * P:(c + 1) * P], ident[:, :])
                    last.then_inc(s["at_ps"], 1)
                if front:
                    x_turn(pe, u, [5])
                if back:
                    wait(pe, s["agT_done"], w, 1, 1)
                    for c in range(CC):
                        last = mm(MI[0][:, 0:C], agT[:, c, :], pj_s[:, c, :], start=(c == 0), stop=(c == CC - 1))
                    last.then_inc(s["pj_ps"], 1)
                if mid:
                    score(pe, v, 3)
                if front:
                    x_turn(pe, u, [6])
                if back:
                    wait(pe, s["xn_done"], w, 1, 1)
                    for c in range(CC):
                        last = pe.transpose(MI[1][:, c * P:(c + 1) * P], xn[:, c * P:(c + 1) * P], ident[:, :])
                    last.then_inc(s["nt_ps"], 1)
                    n = P + 1 if w.two == 0 else P
                    for m in range(CC):
                        o = MI[0][:, m * 256:m * 256 + n]
                        for c in range(CC):
                            mm(o, hh_s[:, c, m * P:(m + 1) * P], hT[w.two][:, c, 0:n], start=(c == 0), stop=False)
                        if m == 0:
                            wait(pe, s["xnT_done"], w, 1, 1)
                        for c in range(CC):
                            last = mm(o, ih_s[:, c, m * P:(m + 1) * P], xnT[:, c, 0:n], start=False, stop=(c == CC - 1))
                    last.then_inc(s["h_ps"], 1)
                if mid:
                    wait(pe, s["sc_done"], v, 1, 1)
                    if front:
                        wait(pe, s["u_done"], u, 4, 2)
                    elif back:
                        wait(pe, s["z_low"], w, 4, 4)
                    pe.transpose(ZB[0][:, 0:P], sc2[:, :, :].rearrange("p g h -> p (g h)"), ident[:, :]).then_inc(s["c_ps"], 1)
                if front:
                    x_turn(pe, u, [7])
                if back:
                    wait(pe, s["hT_done"], w, 2, 2)
                    if front:
                        wait(pe, s["u_done"], u, 4, 3)
                    for c in range(CC):
                        last = pe.transpose(ZB[1][:, c * P:(c + 1) * P], hT[w.two][:, c, 0:P], ident[:, :])
                    last.then_inc(s["ht_ps"], 1)
            over_slots(pe, slot)

        @block.vector
        def _(dve):
            n = [0]

            def chain(ins):
                n[0] += 1
                ins.then_inc(s["prep_dve"], 1)
                dve.wait_ge(s["prep_dve"], n[0])

            dve.wait_ge(s["consts_in"], 16 * NCONST)
            for c in range(CC):
                chain(dve.tensor_scalar(sq[:, c, :], raw_q[:, c, :], lq_w[:, c:c + 1], 1.0 / NPIX, ALU.mult, ALU.mult))
                chain(dve.tensor_scalar(sv[:, c, :], raw_v[:, c, :], lkv_w[:, c:c + 1], None, ALU.mult))
            for c in range(CC):
                chain(dve.tensor_scalar(bq_rep[:, c, :], ident[:, :], 0.0, lq_b[:, c:c + 1], ALU.mult, ALU.add))
            chain(dve.tensor_copy(ident16[:, :], ident[:, :]))
            dve.bn_stats(cst, cls_row[:, :]).then_inc(s["cls_dve"], 1)
            dve.wait_ge(s["cls_dve"], 1)
            dve.bn_aggr(cmv, cst).then_inc(s["cls_dve"], 1)
            dve.wait_ge(s["cls_dve"], 2)
            dve.tensor_scalar(cve, cmv[:, 1:2], EPS, None, ALU.add).then_inc(s["cls_dve"], 1)
            dve.wait_ge(s["cls_pool"], 1)
            dve.tensor_scalar(cxn, cls_row[:, :], cmv[:, 0:1], crs, ALU.subtract, ALU.mult).then_inc(s["cls_dve"], 1)
            dve.wait_ge(s["wk_in"], 64)
            chain(dve.tensor_tensor(stage_wk32, stage_wk, lkv_w_row[:, :].unsqueeze(1).to_broadcast([P, HEADS, C]), ALU.mult))
            dve.wait_ge(s["prep_act"], 3)
            for c in range(CC):
                chain(dve.tensor_scalar(vb_rep[:, c, :], ident[:, :], 0.0, vb_col[:, c:c + 1], ALU.mult, ALU.add))
            chain(dve.tensor_reduce(wk_sum, stage_wk32, X, ALU.add))
            chain(dve.tensor_scalar(wk_mean, wk_sum, -1.0 / C, None, ALU.mult))
            chain(dve.tensor_tensor(stage_wk32, stage_wk32, wk_mean.unsqueeze(2).to_broadcast([P, HEADS, C]), ALU.add))
            chain(dve.tensor_scalar(stage_wk, stage_wk32, WSC, None, ALU.mult))
            chain(dve.tensor_copy(wk_st[:, :, :], stage_wk))
            chain(dve.tensor_tensor(wk_st[64:128, :, :], stage_wk[64:128, :, :], wk_st[64:128, :, :], ALU.subtract))
            dve.wait_ge(s["prep_pe"], 5)
            for i, (w, dst) in enumerate(((sq, wq_s), (sv, cv32))):
                for c in range(CC):
                    chain(dve.tensor_tensor(dst[:, c, :], w[:, c, :], US[i][:, 0:C], ALU.subtract))
            chain(dve.tensor_scalar(wvh[:, :, :], cv32, WSC, None, ALU.mult))
            chain(dve.scalar_tensor_tensor(wvl[:, :, :], cv32, WSC, wvh[:, :, :], ALU.mult, ALU.subtract))
            chain(dve.tensor_copy(mask16[:, :], mask[:, :]))
            chain(dve.tensor_copy(qb_row[:, :], ZB[0][:, 0:C]))
            dve.tensor_tensor(cvec[:, :], ZB[1][:, 0:C], projb_row[:, :], ALU.add).then_inc(s["w_ready_dve"], 1)

            def x_low(dve, u, fills):
                for f in fills:
                    wait(dve, s["xT_done"], u, 8, f + 1)
                    dve.tensor_tensor(xTl[u.x][:, 2 * f:2 * f + 2, :].rearrange("p g c -> p (g c)"), TX[f % 2][:, :],
                                      xTh[u.x][:, 2 * f:2 * f + 2, :].rearrange("p g c -> p (g c)"), ALU.subtract)
                    for i in range(2):
                        ins = dve.bn_stats(st[:, 2 * f + i, :], TX[f % 2][:, i * C:(i + 1) * C])
                    ins.then_inc(s["tx_free"], 1)

            def z_out_low(dve, w, fills):
                for f in fills:
                    wait(dve, s["z_done"], w, 4, f + 1)
                    c, half = f // 2, f % 2
                    dve.scalar_tensor_tensor(zl[:, c, :, half * 64:half * 64 + 64], ZB[f % 2][:, :].rearrange("p (h n) -> p h n", n=64),
                                             1.0 / WSC, zh[:, c, :, half * 64:half * 64 + 64], ALU.mult,
                                             ALU.subtract).then_inc(s["z_low"], 1)

            def unmask(dve, v, f):
                wait(dve, s["s_ps"], v, 2, f + 1)
                dve.tensor_tensor(sm[:, :, :], US[0][:, :].rearrange("p (a t) -> p a t", t=GP),
                                  mask[:, :].unsqueeze(1).to_broadcast([P, G // 2 * HEADS, GP]), ALU.mult).then_inc(s["s_masked"], 1)
                wait(dve, s["s_masked"], v, 2, f + 1)
                dve.tensor_reduce(sc[:, f * 8:f * 8 + 8, :].rearrange("p g h -> p (g h)"), sm[:, :, :], X,
                                  ALU.add).then_inc(s["s_summed"], 1)

            def slot(dve, u, front, mid, back):
                v, w = u.before(), u.before(2)
                if back:
                    wait(dve, s["ex_done"], w, 1, 1)
                    dve.tensor_reduce(den[:, :], ex[:, :, :], X, ALU.add).then_inc(s["p_sum"], 1)
                    wait(dve, s["p_sum"], w, 1, 1)
                    dve.reciprocal(rden[:, :], den[:, :]).then_inc(s["p_rec"], 1)
                    wait(dve, s["p_rec"], w, 1, 1)
                    dve.tensor_tensor(pr[:, :, :], ex[:, :, :], rden[:, :].unsqueeze(2).to_broadcast([P, GP, NPIX]),
                                      ALU.mult).then_inc(s["p_done"], 1)
                if front:
                    wait(dve, s["rT_done"], u, 1, 1)
                    dve.bn_stats(qst[:, :], rT[:, :]).then_inc(s["q_stat"], 1)
                    wait(dve, s["qve_done"], u, 1, 0)
                    wait(dve, s["q_stat"], u, 1, 1)
                    dve.memset(held[:, :], 0.0)
                    dve.bn_aggr(qmv[:, :], qst[:, :]).then_inc(s["q_var"], 1)
                if back:
                    wait(dve, s["pt_ps"], w, 1, 1)
                    dve.scalar_tensor_tensor(pc[:, :, :], ZB[0][:, 0:P].rearrange("p (g h) -> p g h", h=HEADS), WSC,
                                             rs_px[w.two][:, :].unsqueeze(2).to_broadcast([P, G, HEADS]), ALU.mult,
                                             ALU.mult).then_inc(s["pc_done"], 1)
                    wait(dve, s["pc_done"], w, 1, 1)
                    wait(dve, s["pd_done"], w, 2, 0)
                    dve.tensor_copy(pch[:, :, :], pc[:, :, :]).then_inc(s["pc_split"], 1)
                    wait(dve, s["pc_split"], w, 2, 1)
                    dve.tensor_tensor(pcl[:, :, :], pc[:, :, :], pch[:, :, :], ALU.subtract).then_inc(s["pc_split"], 1)
                if front:
                    x_low(dve, u, [0, 1])
                    wait(dve, s["q_ps"], u, 1, 1)
                    wait(dve, s["q_rs_done"], u, 1, 1)
                    dve.scalar_tensor_tensor(q_s[:, :], MI[0][:, 0:C], q_rs[:, 0:1], qb_row[:, :], ALU.mult,
                                             ALU.add).then_inc(s["q_done"], 1)
                    wait(dve, s["q_done"], u, 1, 1)
                    qv = q_s[:, :].rearrange("p (h d) -> p h d", d=D)
                    dve.tensor_copy(qs[:, :, 0, :], qv).then_inc(s["q_split"], 1)
                    wait(dve, s["q_split"], u, 3, 1)
                    dve.tensor_tensor(qs[:, :, 1, :], qv, qs[:, :, 0, :], ALU.subtract).then_inc(s["q_split"], 1)
                    wait(dve, s["q_split"], u, 3, 2)
                    dve.tensor_copy(qs[:, :, 2:4, :], qs[:, :, 0:2, :]).then_inc(s["q_split"], 1)
                if mid:
                    unmask(dve, v, 0)
                if front:
                    x_low(dve, u, [2])
                if back:
                    z_out_low(dve, w, [0, 1])
                if front:
                    x_low(dve, u, [3])
                if back:
                    z_out_low(dve, w, [2, 3])
                if front:
                    x_low(dve, u, [4, 5])
                if back:
                    wait(dve, s["pj_ps"], w, 1, 1)
                    wait(dve, s["rc_done"], w, 1, 1)
                    dve.tensor_tensor(h_s[w.two][:, :], MI[0][:, 0:C], rc[w.x][:, :], ALU.add).then_inc(s["h_done"], 1)
                    wait(dve, s["h_done"], w, 1, 1)
                    dve.bn_stats(hst[:, :], h_s[w.two][:, :]).then_inc(s["h_stat"], 1)
                    wait(dve, s["hve_done"], w, 1, 0)
                    wait(dve, s["h_stat"], w, 1, 1)
                    dve.memset(held[:, :], 0.0)
                    dve.bn_aggr(hmv[:, :], hst[:, :]).then_inc(s["h_var"], 1)
                if mid:
                    unmask(dve, v, 1)
                if back:
                    wait(dve, s["h_rs_done"], w, 1, 1)
                    dve.tensor_scalar(xn[:, :], h_s[w.two][:, :], hmv[:, 0:1], h_rs[:, 0:1], ALU.subtract,
                                      ALU.mult).then_inc(s["xn_done"], 1)
                if mid:
                    wait(dve, s["s_summed"], v, 2, 2)
                    wait(dve, s["rs_px_done"], v, 1, 1)
                    dve.tensor_tensor(sc2[:, :, :], sc[:, :, :], rs_px[v.two][:, :].unsqueeze(2).to_broadcast([P, G, HEADS]),
                                      ALU.mult).then_inc(s["sc_done"], 1)
                if front:
                    x_low(dve, u, [6])
                if mid:
                    wait(dve, s["c_ps"], v, 1, 1)
                    cv = ZB[0][:, 0:P].rearrange("p (t n) -> p t n", n=NPIX)
                    dve.tensor_reduce(mx[:, :], cv, X, ALU.max).then_inc(s["c_max"], 1)
                    wait(dve, s["c_max"], v, 1, 1)
                    dve.tensor_tensor(lg[:, :, :], cv, mx[:, :].unsqueeze(2).to_broadcast([P, GP, NPIX]),
                                      ALU.subtract).then_inc(s["c_sub"], 1)
                if front:
                    x_low(dve, u, [7])
                if back:
                    wait(dve, s["ht_ps"], w, 1, 1)
                    wait(dve, s["h2_out"], w, 16, 0)
                    dve.tensor_tensor(h2[:, :], ZB[1][:, 0:C], h_s[w.two][:, :], ALU.add).then_inc(s["h2_done"], 1)
                if front:
                    wait(dve, s["tx_free"], u, 8, 8)
                    dve.tensor_tensor(v_b[:, :], st[:, :, 1], st[:, :, 4], ALU.subtract).then_inc(s["px_ve_done"], 1)
                    dve.tensor_tensor(v_c[:, :], st[:, :, 2], st[:, :, 5], ALU.add).then_inc(s["px_ve_done"], 1)
                    wait(dve, s["px_ve_done"], u, 2, 2)
                    dve.scalar_tensor_tensor(v_d[:, :], v_b[:, :], C / 4.0, v_b[:, :], ALU.mult, ALU.mult).then_inc(s["px_var"], 1)
                    wait(dve, s["px_var"], u, 3, 1)
                    dve.tensor_tensor(v_a[:, :], v_d[:, :], v_c[:, :], ALU.add).then_inc(s["px_var"], 1)
                    wait(dve, s["px_var"], u, 3, 2)
                    wait(dve, s["rs_px_done"], u, 1, 0)
                    dve.tensor_scalar(v_e[:, :], v_a[:, :], 1.0 / C, EPS, ALU.mult, ALU.add).then_inc(s["px_var"], 1)
            over_slots(dve, slot)

        tokens.close()
        stage_a.close()

        hc = [sb(f"hc{i}", [P, TPC, C]) for i in range(2)]
        tok = [sb(f"tok{i}", [P, TPC, C]) for i in range(2)]
        acc = [sb(f"acc{i}", [P, TPC, C]) for i in range(2)]
        th = [sb(f"th{i}", [P, CC, TPC * P], F16) for i in range(2)]
        tl = [sb(f"tl{i}", [P, CC, TPC * P], F16) for i in range(2)]
        g32 = [sb(f"g32_{i}", [P, CC, TPC * P]) for i in range(2)]
        gh = [sb(f"gh{i}", [P, CC, TPC * P], F16) for i in range(2)]
        gl = [sb(f"gl{i}", [P, CC, TPC * P], F16) for i in range(2)]
        w1h, w1l, w2h, w2l = [sb(n, [P, E, CC, C], F16) for n in ("w1h", "w1l", "w2h", "w2l")]
        WST = 4
        wst = [sb(f"wst{i}", [P, CC, C]) for i in range(WST)]
        est = sb("est", [P, TPC, 6])
        emv = sb("emv", [P, TPC, 2])
        eve = sb("eve", [P, TPC])
        ers = sb("ers", [P, TPC])
        comb = sb("comb", [P, TPC, E])
        combs = [sb(f"combs{i}", [P, TPC, E]) for i in range(2)]
        cT = sb("cT", [E, TPC * P])
        small = {n: sb(n, [P, TPC, E]) for n in "ls le pb eq1 cand1 oh1 p2 eq2 cand2 oh2 ct1 ct2".split()}
        tiny = {n: sb(n, [P, TPC]) for n in "lmx lsum lrec m1 i1 m2 i2 msum mcl mrec rw1 rw2".split()}
        rth = sb("rth", [P, CC, E], F16)
        rtl = sb("rtl", [P, CC, E], F16)
        rt32 = sb("rt32", [P, CC, E])
        b2_s = sb("b2_s", [E, C])
        iota8 = sb("iota8", [P, TPC, E])
        TT, LG, L1, Y = pbank[0:2], pbank[2], pbank[3:5], pbank[5:7]
        CL = pbank[7]
        names = """hc0_in hc1_in w_in ew_in w_hi w_lo rt_scaled rt_hi rt_lo cls_turned cls_h
            e_stat e_var e_ve e_rs tok_done base_done tt_ps th_done tl_done lg_ps le_done route comb_done ct_ps cT_done
            l1_ps g32_done gh_done gl_done y_ps y_done out0_done out1_done""".split()
        s = {n: sem("e_" + n) for n in names}
        w_in = [sem(f"e_wst{i}_in") for i in range(WST)]
        hc_in = [s["hc0_in"], s["hc1_in"]]
        out_done = [s["out0_done"], s["out1_done"]]
        ROUTE = 24
        YF = 2 * (E + 1)

        def over_chunks(eng, chunk):
            chunk(eng, Chunk(0, 0))
            half = (CHUNKS - 2) // 2
            with eng.Fori(0, half) as j:
                for k in (1, 2):
                    chunk(eng, Chunk(j, k))
            chunk(eng, Chunk(half, 1))
            chunk(eng, Chunk(half, 2, True))

        experts = ExitStack()
        block2 = experts.enter_context(nc.Block())

        @block2.sync
        def _(sp):
            chunks_in = h2_dram.rearrange("(n i) p c -> n p i c", i=TPC)

            def load_h(n, k):
                sp.dma_start(hc[k][:, :, :], chunks_in[n]).then_inc(hc_in[k], 16)
            load_h(0, 0)
            load_h(1, 1)
            sp.dma_start(rt32[:, :, :], routerT.rearrange("(c p) e -> p c e", p=P)).then_inc(s["ew_in"], 16)
            sp.dma_start(b2_s[:, :], b2).then_inc(s["ew_in"], 16)
            sp.dma_start(iota8[:, :, :], iota_in.rearrange("p (i e) -> p i e", e=E)).then_inc(s["ew_in"], 16)
            for n in range(2 * E):
                if n >= WST:
                    sp.wait_ge(s["w_lo"], n - WST + 1)
                w = w1 if n % 2 == 0 else w2
                sp.dma_start(wst[n % WST][:, :, :], w[n // 2].rearrange("(c p) n -> p c n", p=P)).then_inc(w_in[n % WST], 16)
            def chunk(sp, ch):
                if ch.last:
                    wait(sp, s["y_done"], ch, YF, E + 1)
                    sp.dma_start(out[:, 0, :], acc[ch.two][0:B, 0, :]).then_inc(out_done[0], 16)
                    return
                n = ch.j * 2 + ch.k
                imgs = [ch.j * (2 * TPC // HALVES) + (ch.k * (TPC // HALVES) + i) for i in range(TPC // HALVES)]
                if not isinstance(n, int):
                    imgs = [sp.snap(i, min_val=0, max_val=B - 1) for i in imgs]
                if not isinstance(n, int) or n + 2 < CHUNKS:
                    m = n + 2 if isinstance(n, int) else sp.snap(n + 2, min_val=0, max_val=CHUNKS - 1)
                    wait_all(sp, [(s["base_done"], ch, 1, 1)])
                    load_h(m, ch.two)
                wait_all(sp, [(s["y_done"], ch, YF, YF)])
                for i, img in enumerate(imgs):
                    sp.dma_start(out[img, 1:TOKS + 1, :].rearrange("(t p) c -> p t c", p=P),
                                 acc[ch.two][:, i * HALVES:(i + 1) * HALVES, :]).then_inc(out_done[ch.two], 16)
            chunk(sp, Chunk(0, 0))
            half = (CHUNKS - 2) // 2
            with sp.Fori(0, half - 1) as j:
                for k in (1, 2):
                    chunk(sp, Chunk(j, k))
            for k in (1, 2):
                chunk(sp, Chunk(half - 1, k))
            chunk(sp, Chunk(half, 1))
            chunk(sp, Chunk(half, 2, True))
            sp.wait_ge(out_done[0], 16 * (B // 2 + 1))
            sp.wait_ge(out_done[1], 16 * (B // 2))

        def wait_h(eng, ch):
            if ch.last:
                eng.wait_ge(s["cls_h"], 1)
            else:
                eng.wait_ge(hc_in[ch.two], ch.j * 16 + (ch.k // 2 + 1) * 16)

        @block2.gpsimd
        def _(pool):
            def prep(pool, ch):
                n, t = ch.rows, ch.tiles
                wait(pool, s["e_ve"], ch, 1, 1)
                pool.tensor_tensor(ers[0:n, 0:t], eve[0:n, 0:t], half_neg[0:n, 0:t], ALU.pow).then_inc(s["e_rs"], 1)
                wait(pool, s["tok_done"], ch, TPC, t)
                stored = (ch.j + ch.k // 2) * (16 * TPC // HALVES)
                if not isinstance(stored, int) or stored > 0:
                    pool.wait_ge(out_done[ch.two], stored)
                pool.tensor_tensor(acc[ch.two][0:n, 0:t, :], hc[ch.two][0:n, 0:t, :], tok[ch.two][0:n, 0:t, :],
                                   ALU.add).then_inc(s["base_done"], 1)
            prep(pool, Chunk(0, 0))

            def chunk(pool, ch):
                if not ch.last:
                    nxt = ch.next()
                    prep(pool, nxt)
            over_chunks(pool, chunk)

        @block2.scalar
        def _(act):
            def turned(act, ch):
                for c in range(CC):
                    wait(act, s["tt_ps"], ch, CC, c + 1)
                    act.activation(th[ch.two][:, c, 0:ch.cols], TT[c][:, 0:ch.cols], ACT.Copy).then_inc(s["th_done"], 1)

            def route_exp(act, ch):
                n, t = ch.rows, ch.tiles
                wait(act, s["route"], ch, ROUTE, 2)
                act.activation(small["le"][0:n, 0:t, :], small["ls"][0:n, 0:t, :], ACT.Exp,
                               scale=1.0 / WSC).then_inc(s["le_done"], 1)

            def gates_turned(act, ch):
                wait(act, s["ct_ps"], ch, 1, 1)
                act.activation(cT[:, 0:ch.cols], TT[0][0:E, 0:ch.cols], ACT.Copy).then_inc(s["cT_done"], 1)

            def gelus(act, ch, e):
                for m in range(CC):
                    wait(act, s["l1_ps"], ch, 2 * E, 2 * e + m + 1)
                    for dst, done in ((g32, "g32_done"), (gh, "gh_done")):
                        act.activation(dst[e % 2][:, m, 0:ch.cols], L1[m][:, 0:ch.cols], ACT.Gelu,
                                       bias=b1_s[:, e, m:m + 1], scale=1.0 / WSC).then_inc(s[done], 1)

            act.wait_ge(s["rt_lo"], 1)
            turned(act, Chunk(0, 0))
            route_exp(act, Chunk(0, 0))
            gates_turned(act, Chunk(0, 0))

            def chunk(act, ch):
                for e in range(E):
                    if not ch.last:
                        if e == 4:
                            turned(act, ch.next())
                        if e == 7:
                            route_exp(act, ch.next())
                    gelus(act, ch, e)
                if not ch.last:
                    gates_turned(act, ch.next())
            over_chunks(act, chunk)

        @block2.tensor
        def _(pe):
            mm = pe.matmul

            def turn(pe, ch):
                n = ch.rows
                wait(pe, s["cT_done"], ch, 1, 0)
                wait(pe, s["tl_done"], ch, CC, 0)
                for c in range(CC):
                    for i in range(ch.tiles):
                        wait(pe, s["tok_done"], ch, TPC, i + 1)
                        last = pe.transpose(TT[c][:, i * n:(i + 1) * n], tok[ch.two][0:n, i, c * P:(c + 1) * P], ident[0:n, 0:n])
                    last.then_inc(s["tt_ps"], 1)

            def logits(pe, ch):
                n = ch.rows
                wait(pe, s["th_done"], ch, CC, CC)
                wait(pe, s["tl_done"], ch, CC, CC)
                for i in range(ch.tiles):
                    o = LG[0:n, i * E:(i + 1) * E]
                    for c in range(CC):
                        for a, t in enumerate((th, tl)):
                            for b, r in enumerate((rth, rtl)):
                                last = mm(o, t[ch.two][:, c, i * n:(i + 1) * n], r[:, c, :], start=(c + a + b == 0),
                                          stop=(c + a + b == CC + 1))
                last.then_inc(s["lg_ps"], 1)

            def gates(pe, ch):
                n = ch.rows
                wait(pe, s["comb_done"], ch, 1, 1)
                for i in range(ch.tiles):
                    last = pe.transpose(TT[0][0:E, i * n:(i + 1) * n], comb[0:n, i, :], ident[0:n, 0:n])
                last.then_inc(s["ct_ps"], 1)

            def first(pe, ch, e):
                for m in range(CC):
                    wait(pe, s["gh_done"], ch, 2 * E, 2 * e + m - 1)
                    o = L1[m][:, 0:ch.cols]
                    for c in range(CC):
                        wh, wl = w1h[:, e, c, m * P:(m + 1) * P], w1l[:, e, c, m * P:(m + 1) * P]
                        xh, xl = th[ch.two][:, c, 0:ch.cols], tl[ch.two][:, c, 0:ch.cols]
                        mm(o, wh, xh, start=(c == 0), stop=False)
                        mm(o, wh, xl, start=False, stop=False)
                        last = mm(o, wl, xh, start=False, stop=(c == CC - 1))
                    last.then_inc(s["l1_ps"], 1)

            def out_fill(pe, ch, step, p):
                f = step * ch.fills + p
                wait(pe, s["y_done"], ch, YF, f - 1)
                return Y[f % 2]

            def bias2(pe, ch):
                n = ch.rows
                wait(pe, s["cT_done"], ch, 1, 1)
                for p in range(ch.fills):
                    bank = out_fill(pe, ch, 0, p)
                    for i in range(2 * p, min(2 * p + 2, ch.tiles)):
                        last = mm(bank[0:n, (i % 2) * C:(i % 2 + 1) * C], cT[:, i * n:(i + 1) * n], b2_s[:, :], start=True, stop=True)
                    last.then_inc(s["y_ps"], 1)

            def second(pe, ch, e):
                n = ch.rows
                wait(pe, s["gh_done"], ch, 2 * E, 2 * e + 2)
                wait(pe, s["gl_done"], ch, 2 * E, 2 * e + 2)
                for p in range(ch.fills):
                    bank = out_fill(pe, ch, e + 1, p)
                    for i in range(2 * p, min(2 * p + 2, ch.tiles)):
                        o = bank[0:n, (i % 2) * C:(i % 2 + 1) * C]
                        for c in range(CC):
                            hi, lo = gh[e % 2][:, c, i * n:(i + 1) * n], gl[e % 2][:, c, i * n:(i + 1) * n]
                            mm(o, hi, w2h[:, e, c, :], start=(c == 0), stop=False)
                            mm(o, hi, w2l[:, e, c, :], start=False, stop=False)
                            last = mm(o, lo, w2h[:, e, c, :], start=False, stop=(c == CC - 1))
                    last.then_inc(s["y_ps"], 1)

            for c in range(CC):
                last = pe.transpose(CL[0:B, c * P:(c + 1) * P], clsH[:, c, :], ident[:, :])
            last.then_inc(s["cls_turned"], 1)
            turn(pe, Chunk(0, 0))
            pe.wait_ge(s["rt_lo"], 1)
            logits(pe, Chunk(0, 0))
            gates(pe, Chunk(0, 0))

            def chunk(pe, ch):
                zero = isinstance(ch.j, int) and ch.j == 0 and ch.k == 0
                for e in range(E):
                    if zero:
                        pe.wait_ge(s["w_lo"], 2 * e + 2)
                    first(pe, ch, e)
                    if e == 0:
                        pe.wait_ge(s["ew_in"], 48)
                        bias2(pe, ch)
                    else:
                        second(pe, ch, e - 1)
                    if not ch.last:
                        if e == 3:
                            turn(pe, ch.next())
                        if e == 5:
                            logits(pe, ch.next())
                        if e == 7:
                            gates(pe, ch.next())
                second(pe, ch, E - 1)
            over_chunks(pe, chunk)

        @block2.vector
        def _(dve):
            def stats(dve, ch):
                n = ch.rows
                wait_h(dve, ch)
                for i in range(ch.tiles):
                    dve.bn_stats(est[0:n, i, :], hc[ch.two][0:n, i, :]).then_inc(s["e_stat"], 1)
                wait(dve, s["e_stat"], ch, TPC, ch.tiles)
                dve.memset(held[:, :], 0.0)
                for i in range(ch.tiles):
                    dve.bn_aggr(emv[0:n, i, :], est[0:n, i, :]).then_inc(s["e_var"], 1)
                wait(dve, s["e_var"], ch, TPC, ch.tiles)
                dve.tensor_scalar(eve[0:n, 0:ch.tiles], emv[0:n, 0:ch.tiles, 1], EPS, None, ALU.add).then_inc(s["e_ve"], 1)

            def normal(dve, ch):
                n = ch.rows
                wait(dve, s["e_rs"], ch, 1, 1)
                for i in range(ch.tiles):
                    dve.tensor_scalar(tok[ch.two][0:n, i, :], hc[ch.two][0:n, i, :], emv[0:n, i, 0:1], ers[0:n, i:i + 1],
                                      ALU.subtract, ALU.mult).then_inc(s["tok_done"], 1)

            def low(dve, ch):
                for c in range(CC):
                    wait(dve, s["th_done"], ch, CC, c + 1)
                    dve.tensor_tensor(tl[ch.two][:, c, 0:ch.cols], TT[c][:, 0:ch.cols], th[ch.two][:, c, 0:ch.cols],
                                      ALU.subtract).then_inc(s["tl_done"], 1)

            def route(dve, ch, part):
                n, t = ch.rows, ch.tiles
                S = {k: a[0:n, 0:t, :] for k, a in small.items()}
                T = {k: a[0:n, 0:t] for k, a in tiny.items()}
                over = lambda a: a.unsqueeze(2).to_broadcast([n, t, E])
                io = iota8[0:n, 0:t, :]
                count = [2 * part]

                def step(ins):
                    count[0] += 1
                    ins.then_inc(s["route"], 1)
                    wait(dve, s["route"], ch, ROUTE, count[0])

                lg = LG[0:n, 0:t * E].rearrange("p (t e) -> p t e", e=E)
                wait(dve, s["lg_ps"], ch, 1, 1)
                if part == 0:
                    step(dve.tensor_reduce(T["lmx"], lg, X, ALU.max))
                    step(dve.tensor_tensor(S["ls"], lg, over(T["lmx"]), ALU.subtract))
                    return
                wait(dve, s["le_done"], ch, 1, 1)
                step(dve.tensor_reduce(T["lsum"], S["le"], X, ALU.add))
                step(dve.reciprocal(T["lrec"], T["lsum"]))
                step(dve.tensor_tensor(S["pb"], S["le"], over(T["lrec"]), ALU.mult))
                for prob, m, eq, cand, i, oh in (("pb", "m1", "eq1", "cand1", "i1", "oh1"), ("p2", "m2", "eq2", "cand2", "i2", "oh2")):
                    step(dve.tensor_reduce(T[m], S[prob], X, ALU.max))
                    step(dve.tensor_tensor(S[eq], S[prob], over(T[m]), ALU.is_equal))
                    step(dve.tensor_tensor(S[cand], S[eq], io, ALU.mult))
                    step(dve.tensor_reduce(T[i], S[cand], X, ALU.min))
                    step(dve.tensor_tensor(S[oh], io, over(T[i]), ALU.is_equal))
                    if prob == "pb":
                        step(dve.scalar_tensor_tensor(S["p2"], S["oh1"], -4.0, S["pb"], ALU.mult, ALU.add))
                step(dve.tensor_tensor(T["msum"], T["m1"], T["m2"], ALU.add))
                step(dve.tensor_scalar(T["mcl"], T["msum"], 1e-12, None, ALU.max))
                step(dve.reciprocal(T["mrec"], T["mcl"]))
                step(dve.tensor_tensor(T["rw1"], T["m1"], T["mrec"], ALU.mult))
                step(dve.tensor_tensor(T["rw2"], T["m2"], T["mrec"], ALU.mult))
                step(dve.tensor_tensor(S["ct1"], S["oh1"], over(T["rw1"]), ALU.mult))
                step(dve.tensor_tensor(S["ct2"], S["oh2"], over(T["rw2"]), ALU.mult))
                wait(dve, s["ct_ps"], ch, 1, 0)
                step(dve.tensor_tensor(comb[0:n, 0:t, :], S["ct1"], S["ct2"], ALU.add))
                assert count[0] == ROUTE
                dve.tensor_scalar(combs[ch.two][0:n, 0:t, :], comb[0:n, 0:t, :], 1.0 / WSC, None, ALU.mult)\
                   .then_inc(s["comb_done"], 1)

            def gelu_low(dve, ch, e):
                for m in range(CC):
                    wait(dve, s["g32_done"], ch, 2 * E, 2 * e + m + 1)
                    wait(dve, s["gh_done"], ch, 2 * E, 2 * e + m + 1)
                    dve.tensor_tensor(gl[e % 2][:, m, 0:ch.cols], g32[e % 2][:, m, 0:ch.cols], gh[e % 2][:, m, 0:ch.cols],
                                      ALU.subtract).then_inc(s["gl_done"], 1)

            def add_out(dve, ch, step):
                n = ch.rows
                a = acc[ch.two]
                for p in range(ch.fills):
                    f = step * ch.fills + p
                    wait(dve, s["y_ps"], ch, YF, f + 1)
                    if step == 0:
                        wait(dve, s["base_done"], ch, 1, 1)
                        k = min(2, ch.tiles)
                        ins = dve.tensor_tensor(a[0:n, 2 * p:2 * p + k, :].rearrange("p t c -> p (t c)"), Y[f % 2][0:n, 0:k * C],
                                                a[0:n, 2 * p:2 * p + k, :].rearrange("p t c -> p (t c)"), ALU.add)
                    else:
                        e = step - 1
                        wait(dve, s["comb_done"], ch, 1, 1)
                        wait(dve, s["y_done"], ch, YF, f - ch.fills + 1)
                        for i in range(2 * p, min(2 * p + 2, ch.tiles)):
                            ins = dve.scalar_tensor_tensor(a[0:n, i, :], Y[f % 2][0:n, (i % 2) * C:(i % 2 + 1) * C],
                                                           combs[ch.two][0:n, i, e:e + 1], a[0:n, i, :], ALU.mult, ALU.add)
                    ins.then_inc(s["y_done"], 1)

            def prep(dve, ch):
                stats(dve, ch)
                normal(dve, ch)

            prep(dve, Chunk(0, 0))
            dve.wait_ge(s["ew_in"], 48)
            dve.tensor_scalar(rt32[:, :, :], rt32[:, :, :], WSC, None, ALU.mult).then_inc(s["rt_scaled"], 1)
            dve.wait_ge(s["rt_scaled"], 1)
            dve.tensor_copy(rth[:, :, :], rt32[:, :, :]).then_inc(s["rt_hi"], 1)
            dve.wait_ge(s["rt_hi"], 1)
            dve.tensor_tensor(rtl[:, :, :], rt32[:, :, :], rth[:, :, :], ALU.subtract).then_inc(s["rt_lo"], 1)
            low(dve, Chunk(0, 0))
            route(dve, Chunk(0, 0), 0)
            route(dve, Chunk(0, 0), 1)

            def split(n):
                e = n // 2
                hi, lo = (w1h, w1l) if n % 2 == 0 else (w2h, w2l)
                dve.wait_ge(w_in[n % WST], 16 * (n // WST + 1))
                dve.tensor_scalar(hi[:, e, :, :], wst[n % WST][:, :, :], WSC, None, ALU.mult).then_inc(s["w_hi"], 1)
                dve.wait_ge(s["w_hi"], n + 1)
                dve.scalar_tensor_tensor(lo[:, e, :, :], wst[n % WST][:, :, :], WSC, hi[:, e, :, :], ALU.mult,
                                         ALU.subtract).then_inc(s["w_lo"], 1)

            def chunk(dve, ch):
                zero = isinstance(ch.j, int) and ch.j == 0 and ch.k == 0
                for e in range(E):
                    if zero:
                        split(2 * e)
                        split(2 * e + 1)
                    gelu_low(dve, ch, e)
                    add_out(dve, ch, e)
                    if not ch.last:
                        if e == 1:
                            if ch.next().last:
                                dve.wait_ge(s["cls_turned"], 1)
                                wait(dve, s["base_done"], ch, 1, 0)
                                dve.tensor_tensor(hc[0][0:B, 0, :], CL[0:B, 0:C], cls_row[:, :], ALU.add).then_inc(s["cls_h"], 1)
                            stats(dve, ch.next())
                        if e == 2:
                            normal(dve, ch.next())
                        if e == 4:
                            low(dve, ch.next())
                        if e == 5:
                            route(dve, ch.next(), 0)
                        if e == 6:
                            route(dve, ch.next(), 1)
                add_out(dve, ch, E)
            over_chunks(dve, chunk)
        experts.close()


def kernel(x, cls_tok, L0_tok_ln_q_w, L0_tok_ln_q_b, L0_tok_Wq, L0_tok_ln_kv_w, L0_tok_ln_kv_b, L0_tok_Wkv,
           L0_tok_proj_w, L0_tok_proj_b, L0_attn_W_ih, L0_attn_W_hh, L0_attn_b_ih, L0_attn_b_hh,
           L0_ffn_router_w, L0_ffn_w1, L0_ffn_b1, L0_ffn_w2, L0_ffn_b2):
    import numpy as np
    import concourse.bacc as bacc
    from concourse import mybir as mb
    from concourse.bass_utils import run_bass_kernel_spmd

    h = IMG // STRIDE
    xg = np.asarray(x).reshape(B, C // P, P, h, STRIDE, h, STRIDE).transpose(0, 3, 2, 1, 5, 4, 6)
    xg = xg.reshape(B, HALVES, h // HALVES, P, C // P, h, NPIX).transpose(0, 1, 3, 4, 2, 5, 6).reshape(UNITS, P, C // P, PIX)
    pix = np.arange(P)

    def col(a):
        return np.asarray(a).reshape(C // P, P).T

    arrays = {
        "xg": xg, "cls_tok": np.asarray(cls_tok).reshape(C),
        "ln_q_w": col(L0_tok_ln_q_w), "ln_q_b": col(L0_tok_ln_q_b), "wqT": np.asarray(L0_tok_Wq).T,
        "ln_kv_w": L0_tok_ln_kv_w, "ln_kv_w_col": col(L0_tok_ln_kv_w), "ln_kv_b": col(L0_tok_ln_kv_b),
        "wk": np.asarray(L0_tok_Wkv)[:C], "wvT": np.asarray(L0_tok_Wkv)[C:].T,
        "projT": np.asarray(L0_tok_proj_w).T, "proj_b": L0_tok_proj_b,
        "wihT": np.asarray(L0_attn_W_ih).T, "whhT": np.asarray(L0_attn_W_hh).T,
        "b_ih": col(L0_attn_b_ih), "b_hh": col(L0_attn_b_hh),
        "routerT": np.asarray(L0_ffn_router_w).T, "w1": L0_ffn_w1,
        "b1": np.asarray(L0_ffn_b1).reshape(E * (C // P), P).T, "w2": L0_ffn_w2, "b2": L0_ffn_b2,
        "ident_in": np.eye(P, dtype=np.float32),
        "mask_in": (pix[:, None] // NPIX == np.arange(GP)[None, :]).astype(np.float32),
        "iota_in": np.tile(np.arange(E, dtype=np.float32) - E, (P, TPC)),
    }
    arrays = {k: np.ascontiguousarray(v) for k, v in arrays.items()}
    nc = bacc.Bacc("TRN2", target_bir_lowering=False, num_devices=1)
    args = [nc.dram_tensor(k, v.shape, mb.dt.from_np(v.dtype), kind="ExternalInput").ap() for k, v in arrays.items()]
    out = nc.dram_tensor("tower_out", (B, TOKS + 1, C), mb.dt.from_np(np.dtype("float32")), kind="ExternalOutput").ap()
    vit_tower(nc, *args, out)
    r = run_bass_kernel_spmd(nc, [arrays], core_ids=[0])
    return r.results[0]["tower_out"]
```

```python
from contextlib import ExitStack

import concourse.bass as bass
from concourse import mybir

P = 128
F32 = mybir.dt.float32
F16 = mybir.dt.float16
ALU = mybir.AluOpType
ACT = mybir.ActivationFunctionType
X = mybir.AxisListType.X

B, C, IMG, STRIDE = 32, 256, 64, 4
HEADS, E = 8, 8
NPIX = STRIDE * STRIDE
D = C // HEADS
CC = C // P
TOKS = (IMG // STRIDE) ** 2
UNITS = B * TOKS // P
HALVES = TOKS // P
GP = P // NPIX
G = P // GP
PIX = P * NPIX
XBUF = 4
BN_FILLS = [(1, 5)]
SQ_FILLS = [0, 6, 7]
PT = 64
WSC = 64.0
EPS = 1e-5
TPC = 4
CHUNKS = UNITS // TPC


class Turn:

    width = 1

    def __init__(self, j, k):
        self.j, self.k = j, k
        self.two = k % 2

    def count(self, per, plus):
        return self.j * (self.width * per) + (self.k * per + plus)


class Unit(Turn):

    width = XBUF

    def __init__(self, j, k):
        super().__init__(j, k)
        self.x = k % XBUF

    def before(self, n=1):
        return Unit(self.j, self.k - n)


class Chunk(Turn):

    width = 2

    def __init__(self, j, k, last=False):
        super().__init__(j, k)
        self.last = last
        self.tiles = 1 if last else TPC
        self.rows = B if last else P
        self.cols = self.tiles * self.rows
        self.fills = (self.tiles + 1) // 2

    def next(self):
        return Chunk(self.j, self.k + 1, isinstance(self.j, int) and self.j * 2 + self.k + 1 == CHUNKS)


def wait(eng, sem, unit, per, plus):
    v = unit.count(per, plus)
    if isinstance(v, int) and v <= 0:
        return
    eng.wait_ge(sem, v)


def wait_all(eng, waits):
    values = [(sem, unit.count(per, plus)) for sem, unit, per, plus in waits]
    for _, v in values:
        eng.compute_val(v)
    for sem, v in values:
        if not isinstance(v, int) or v > 0:
            eng.wait_ge(sem, v)


def over_slots(eng, slot, spare=0):
    last = UNITS // XBUF - 1
    for k in range(XBUF):
        slot(eng, Unit(0, k), True, k >= 1, k >= 2, k >= 3)
    with eng.Fori(0, last - spare) as j:
        for k in range(XBUF, 2 * XBUF):
            slot(eng, Unit(j, k), True, True, True, True)
    for n in range(spare):
        for k in range(XBUF, 2 * XBUF):
            slot(eng, Unit(last - spare + n, k), True, True, True, True)
    for k in range(3):
        slot(eng, Unit(last, XBUF + k), False, k < 1, k < 2, True)


def vit_tower(nc, xg, cls_tok, ln_q_w, ln_q_b, wqT, ln_kv_w, ln_kv_w_col, ln_kv_b, wk, wvT, projT, proj_b,
              wihT, whhT, b_ih, b_hh, routerT, w1, b1, w2, b2, ident_in, mask_in, iota_in, out):
    h2_dram = nc.dram_tensor("h2_dram", [UNITS, P, C], F32, kind="Internal").ap()
    ctx = ExitStack()
    with ctx:
        def sb(name, shape, dt=F32):
            return ctx.enter_context(nc.sbuf_tensor(name, shape, dt))

        def sem(name):
            return ctx.enter_context(nc.semaphore(name))

        ident = sb("ident", [P, P])
        ident16 = sb("ident16", [P, P], F16)
        mask16 = sb("mask16", [P, GP], F16)
        mask = sb("mask", [P, GP])
        avg = sb("avg", [P, P])
        lq_w = sb("lq_w", [P, CC])
        lq_b = sb("lq_b", [P, CC])
        lkv_w = sb("lkv_w", [P, CC])
        lkv_b = sb("lkv_b", [P, CC])
        bih_c = sb("bih_c", [P, CC])
        bhh_c = sb("bhh_c", [P, CC])
        rnn_b = sb("rnn_b", [P, CC])
        cls_row = sb("cls_row", [B, C])
        wq_s = sb("wq_s", [P, CC, C])
        wvh = sb("wvh", [P, CC, C], F16)
        wvl = sb("wvl", [P, CC, C], F16)
        pj_s = sb("pj_s", [P, CC, C])
        ih_s = sb("ih_s", [P, CC, C])
        hh_s = sb("hh_s", [P, CC, C])
        qb_row = sb("qb_row", [P, C])
        cvec = sb("cvec", [P, C])
        wk_st = sb("wk_st", [P, HEADS, C], F16)
        eps_c = sb("eps_c", [P, 1])
        held = sb("held", [P, 1])
        half_neg = sb("half_neg", [P, G])
        b1_s = sb("b1_s", [P, E, CC])
        clsH = sb("clsH", [P, CC, B])

        stage_a = ExitStack()
        def sa(name, shape, dt=F32):
            return stage_a.enter_context(nc.sbuf_tensor(name, shape, dt))
        x_s = [sa(f"x{i}", [P, CC, PIX]) for i in range(XBUF)]
        xTh = [sa(f"xTh{i}", [P, G, C], F16) for i in range(XBUF)]
        xTl = [sa(f"xTl{i}", [P, G, C], F16) for i in range(XBUF)]
        r_s = [sa(f"r{i}", [P, CC, P]) for i in range(2)]
        rT = sa("rT", [P, C])
        rc = [sa(f"rc{i}", [P, C]) for i in range(XBUF)]
        add8 = sa("add8", [P, PT, 8])
        add4 = sa("add4", [P, PT, 4])
        add2 = sa("add2", [P, PT, 2])
        q_s = sa("q_s", [P, C])
        qs = sa("qs", [P, HEADS, 4, D], F16)
        qsT = sa("qsT", [P, HEADS, P], F16)
        u_s = [sa(f"u{i}", [P, CC, HEADS, P]) for i in range(2)]
        zh = sa("zh", [P, CC, HEADS, P], F16)
        zl = sa("zl", [P, CC, HEADS, P], F16)
        sm = sa("sm", [P, G // 2 * HEADS, GP])
        sc = sa("sc", [P, G, HEADS])
        sc2 = sa("sc2", [P, G, HEADS])
        mx = sa("mx", [P, GP])
        lg = sa("lg", [P, GP, NPIX])
        ex = sa("ex", [P, GP, NPIX])
        den = sa("den", [P, GP])
        rden = sa("rden", [P, GP])
        pr = sa("pr", [P, GP, NPIX])
        pc = sa("pc", [P, G, HEADS])
        pch = sa("pch", [P, G, HEADS], F16)
        pcl = sa("pcl", [P, G, HEADS], F16)
        pdh = sa("pdh", [P, G, HEADS, GP], F16)
        pdl = sa("pdl", [P, G, HEADS, GP], F16)
        st = sa("st", [P, G, 6])
        v_a = sa("v_a", [P, G])
        x_sum = sa("x_sum", [P, G])
        x_neg = sa("x_neg", [P, G])
        x_sq = sa("x_sq", [P, 2, C])
        v_b = sa("v_b", [P, G])
        v_c = sa("v_c", [P, G])
        v_d = sa("v_d", [P, G])
        v_e = sa("v_e", [P, G])
        rs_px = [sa(f"rs_px{i}", [P, G]) for i in range(2)]
        qst = sa("qst", [P, 6])
        qmv = sa("qmv", [P, 2])
        qve = sa("qve", [P, 1])
        q_rs = sa("q_rs", [P, 1])
        ag = sa("ag", [P, C])
        agT = sa("agT", [P, CC, P])
        h_s = sa("h_s", [P, C])
        hst = sa("hst", [P, 6])
        hmv = sa("hmv", [P, 2])
        hve = sa("hve", [P, 1])
        h_rs = sa("h_rs", [P, 1])
        xn = sa("xn", [P, C])
        xnT = sa("xnT", [P, CC, P + 1])
        hT = [sa(f"hT{i}", [P, CC, P + 1]) for i in range(2)]
        h2 = sa("h2", [P, C])

        pbank = [ctx.enter_context(nc.psum_tensor(f"bank{i}", [P, 512], F32)) for i in range(8)]
        TX, US, ZB, MI = pbank[0:2], pbank[2:4], pbank[4:6], pbank[6:8]

        names = """consts_in wk_in cls_in prep_in x0_in x1_in x2_in x3_in
            avg_set prep_pe prep_act prep_dve prep_pool cls_pe cls_dve cls_act cls_pool w_ready_dve w_ready_act
            pool_adds r_done qve_done q_rs_done rc_done px_ve_done rs_px_done h_rs_done pd_done clsH_done hve_done
            z_low pc_split tx_free px_sq px_ss xs_sum xs_neg xs_sq
            rT_ps q_ps qs_ps u_ps xT_ps s_ps c_ps pt_ps z_ps a_ps at_ps pj_ps nt_ps h_ps ht_ps
            rT_done xT_done u_done z_done ag_done agT_done ex_done xnT_done hT_done
            q_stat q_var q_done q_split qsT_done st_done px_var s_masked s_summed sc_done c_max c_sub
            p_sum p_rec p_done pc_done h_done h_stat h_var xn_done h2_done h2_out""".split()
        s = {n: sem(n) for n in names}
        x_in = [s["x0_in"], s["x1_in"], s["x2_in"], s["x3_in"]]

        stage_wk = x_s[1][:, :, :].rearrange("p c (h n) -> p (c h) n", n=C)[:, 0:HEADS, :]
        stage_wk32 = x_s[1][:, :, :].rearrange("p c (h n) -> p (c h) n", n=C)[:, HEADS:2 * HEADS, :]
        stage = x_s[2][:, :, :].rearrange("p c (h n) -> p (c h) n", n=C)
        raw_q, raw_v, sq, sv, cv32 = [stage[:, n * CC:(n + 1) * CC, :] for n in range(5)]
        bq_rep = stage[:, 10, :].rearrange("p (c n) -> p c n", n=P)
        vb_rep = stage[:, 11, :].rearrange("p (c n) -> p c n", n=P)
        vb_col, wk_sum, wk_mean = stage[:, 12, 0:CC], stage[:, 12, 8:8 + HEADS], stage[:, 12, 16:16 + HEADS]
        cst, cmv, cve, crs = [stage[0:B, 13, a:b] for a, b in ((0, 6), (8, 10), (12, 13), (16, 17))]
        cxn = stage[0:B, 14, :]
        lkv_w_row = stage[:, 15, :]
        projb_row = u_s[1][:, 0, 0:C // P, :].rearrange("p a n -> p (a n)")

        NCONST = 17
        tokens = ExitStack()
        block = tokens.enter_context(nc.Block())

        def sync_prep(sp):
            row = lambda a, n: a.partition_broadcast(n)
            loads = [(ident[:, :], ident_in), (mask[:, :], mask_in),
                     (lq_w[:, :], ln_q_w), (lq_b[:, :], ln_q_b),
                     (lkv_w[:, :], ln_kv_w_col), (lkv_b[:, :], ln_kv_b),
                     (bih_c[:, :], b_ih), (bhh_c[:, :], b_hh),
                     (projb_row[:, :], row(proj_b, P)), (lkv_w_row[:, :], row(ln_kv_w, P)),
                     (cls_row[:, :], row(cls_tok, B)),
                     (raw_q, wqT.rearrange("(c p) n -> p c n", p=P)),
                     (raw_v, wvT.rearrange("(c p) n -> p c n", p=P)),
                     (pj_s[:, :, :], projT.rearrange("(c p) n -> p c n", p=P)),
                     (ih_s[:, :, :], wihT.rearrange("(c p) n -> p c n", p=P)),
                     (hh_s[:, :, :], whhT.rearrange("(c p) n -> p c n", p=P)),
                     (b1_s[:, :, :], b1.rearrange("p (e c) -> p e c", e=E))]
            assert len(loads) == NCONST
            for dst, src in loads:
                sp.dma_start(dst, src).then_inc(s["consts_in"], 16)
            for rep in range(4):
                sp.dma_start(stage_wk[rep * D:(rep + 1) * D, :, :],
                             wk.rearrange("(h d) n -> d h n", d=D)).then_inc(s["wk_in"], 16)

        def load_x(sp, u, ahead):
            n = u.j * XBUF + (u.k + ahead)
            n = n if isinstance(n, int) else sp.snap(n, min_val=0, max_val=UNITS - 1)
            t = Unit(u.j, u.k + ahead - XBUF)
            if not (isinstance(t.j, int) and t.j * XBUF + t.k < 0):
                wait_all(sp, [(s["xT_ps"], t, 8, 8), (s["s_ps"], t, 2, 2), (s["r_done"], t, 1, 1)])
            k = (u.k + ahead) % XBUF
            sp.dma_start(x_s[k][:, :, :], xg[n]).then_inc(x_in[k], 16)

        def wait_x(eng, u):
            eng.wait_ge(x_in[u.x], u.j * 16 + (u.k // XBUF + 1) * 16)

        @block.sync
        def _(sp):
            sync_prep(sp)
            sp.dma_start(x_s[0][:, :, :], xg[0]).then_inc(x_in[0], 16)
            sp.dma_start(x_s[3][:, :, :], xg[3]).then_inc(x_in[3], 16)
            sp.wait_ge(s["w_ready_dve"], 1)
            sp.wait_ge(s["w_ready_act"], 1)
            for n in (1, 2):
                sp.dma_start(x_s[n][:, :, :], xg[n]).then_inc(x_in[n], 16)

            def slot(sp, u, front, mid, back, end):
                v, z = u.before(), u.before(3)
                if mid:
                    t = v.j * XBUF + v.k
                    if not isinstance(t, int) or t + XBUF < UNITS:
                        load_x(sp, v, XBUF)
                if end:
                    n = z.j * XBUF + z.k
                    n = n if isinstance(n, int) else sp.snap(n, min_val=0, max_val=UNITS - 1)
                    wait_all(sp, [(s["h2_done"], z, 1, 1)])
                    sp.dma_start(h2_dram[n], h2[:, :]).then_inc(s["h2_out"], 16)
            over_slots(sp, slot, 1)
            sp.wait_ge(s["h2_out"], 16 * UNITS)

        @block.gpsimd
        def _(pool):
            pool.memset(avg[:, :], 1.0 / C).then_inc(s["avg_set"], 1)
            pool.memset(half_neg[:, :], -0.5).then_inc(s["avg_set"], 1)
            pool.memset(eps_c[:, :], EPS).then_inc(s["avg_set"], 1)
            for i in range(2):
                pool.memset(hT[i][:, :, :], 0.0).then_inc(s["avg_set"], 1)
            pool.memset(xnT[:, :, :], 0.0).then_inc(s["avg_set"], 1)
            pool.wait_ge(s["avg_set"], 6)
            pool.wait_ge(s["cls_dve"], 3)
            pool.tensor_tensor(crs, cve, half_neg[0:B, 0:1], ALU.pow).then_inc(s["cls_pool"], 1)

            STEPS = CC * P // PT

            def pooling(pool, u, c, q, q0):
                xv = x_s[u.x][:, c, :].rearrange("p (t n) -> p t n", n=NPIX)[:, q * PT:(q + 1) * PT, :]
                base = 3 * q0
                pool.tensor_tensor(add8[:, :, :], xv[:, :, 0:8], xv[:, :, 8:16], ALU.add).then_inc(s["pool_adds"], 1)
                wait(pool, s["pool_adds"], u, 3 * STEPS, base + 1)
                pool.tensor_tensor(add4[:, :, :], add8[:, :, 0:4], add8[:, :, 4:8], ALU.add).then_inc(s["pool_adds"], 1)
                wait(pool, s["pool_adds"], u, 3 * STEPS, base + 2)
                pool.tensor_tensor(add2[:, :, :], add4[:, :, 0:2], add4[:, :, 2:4], ALU.add).then_inc(s["pool_adds"], 1)
                wait(pool, s["pool_adds"], u, 3 * STEPS, base + 3)
                i = pool.tensor_tensor(r_s[u.two][:, c, q * PT:(q + 1) * PT], add2[:, :, 0], add2[:, :, 1], ALU.add)
                if q0 == STEPS - 1:
                    i.then_inc(s["r_done"], 1)

            def pool_part(pool, u, parts):
                for n in parts:
                    if n == 0:
                        wait_x(pool, u)
                        wait(pool, s["q_ps"], u, 1, -1)
                    pooling(pool, u, n // (P // PT), n % (P // PT), n)

            pool_part(pool, Unit(0, 0), range(STEPS))

            def slot(pool, u, front, mid, back, end):
                v, w, z = u.before(), u.before(2), u.before(3)
                nxt = Unit(u.j, u.k + 1)
                more = front and not (isinstance(u.j, int) and u.j * XBUF + u.k + 1 >= UNITS)
                if mid:
                    wait(pool, s["px_var"], v, 1, 1)
                    pool.tensor_tensor(rs_px[v.two][:, :], v_e[:, :], half_neg[:, :], ALU.pow).then_inc(s["rs_px_done"], 1)
                if front:
                    wait(pool, s["q_var"], u, 1, 1)
                    pool.tensor_tensor(qve[:, :], qmv[:, 1:2], eps_c[:, :], ALU.add).then_inc(s["qve_done"], 1)
                    wait(pool, s["qve_done"], u, 1, 1)
                    pool.tensor_tensor(q_rs[:, :], qve[:, :], half_neg[:, 0:1], ALU.pow).then_inc(s["q_rs_done"], 1)
                if back:
                    wait(pool, s["pc_split"], w, 2, 2)
                    for part, dst in ((pch, pdh), (pcl, pdl)):
                        pool.tensor_tensor(dst[:, :, :, :].rearrange("p g h t -> p (g h) t"),
                                           part[:, :, :].rearrange("p g h -> p (g h)").unsqueeze(2).to_broadcast([P, G * HEADS, GP]),
                                           mask16[:, :].unsqueeze(1).to_broadcast([P, G * HEADS, GP]),
                                           ALU.mult).then_inc(s["pd_done"], 1)
                if front:
                    wait(pool, s["rT_done"], u, 1, 1)
                    if isinstance(u.j, int) and u.j * XBUF + u.k == 0:
                        pool.wait_ge(s["w_ready_dve"], 1)
                    wait(pool, s["h_done"], u, 1, -3)
                    pool.tensor_tensor(rc[u.x][:, :], rT[:, :], cvec[:, :], ALU.add).then_inc(s["rc_done"], 1)
                if end:
                    wait(pool, s["h_var"], z, 1, 1)
                    pool.tensor_tensor(hve[:, :], hmv[:, 1:2], eps_c[:, :], ALU.add).then_inc(s["hve_done"], 1)
                    wait(pool, s["hve_done"], z, 1, 1)
                    pool.tensor_tensor(h_rs[:, :], hve[:, :], half_neg[:, 0:1], ALU.pow).then_inc(s["h_rs_done"], 1)
                if more:
                    pool_part(pool, nxt, range(STEPS))
                if end and z.two == 0:
                    wait(pool, s["hT_done"], z, 2, 2)
                    b = z.j * HALVES + z.k // HALVES
                    pool.tensor_copy(clsH[:, :, bass.ds(b, 1)], hT[0][:, :, P:P + 1]).then_inc(s["clsH_done"], 1)
            over_slots(pool, slot, 1)

        @block.scalar
        def _(act):
            act.wait_ge(s["consts_in"], 16 * NCONST)
            act.wait_ge(s["avg_set"], 6)
            act.activation(rnn_b[:, 0:1], bih_c[:, 0:1], ACT.Identity, bias=bhh_c[:, 0:1]).then_inc(s["prep_act"], 1)
            act.activation(rnn_b[:, 1:2], bih_c[:, 1:2], ACT.Identity, bias=bhh_c[:, 1:2]).then_inc(s["prep_act"], 1)
            act.wait_ge(s["prep_pe"], 3)
            act.activation(vb_col, MI[0][:, 0:CC], ACT.Copy).then_inc(s["prep_act"], 1)
            act.wait_ge(s["cls_pe"], 1)
            act.activation(xnT[:, :, P:P + 1], MI[1][:, 0:CC * B].rearrange("p (c b) -> p c b", b=B)[:, :, 0:1],
                           ACT.Copy).then_inc(s["w_ready_act"], 1)

            def x_out(act, u, fills):
                for f in fills:
                    wait(act, s["xT_ps"], u, 8, f + 1)
                    if f in SQ_FILLS:
                        n, gs = SQ_FILLS.index(f), slice(2 * f, 2 * f + 2)
                        for i in range(2):
                            g = 2 * f + i
                            act.activation(xTh[u.x][:, g, :], TX[f % 2][:, i * C:(i + 1) * C], ACT.Copy,
                                           accum_out=x_sum[:, g:g + 1]).then_inc(s["xs_sum"], 1)
                        wait(act, s["xs_sum"], u, 2 * len(SQ_FILLS), 2 * n + 2)
                        act.activation(x_neg[:, gs], x_sum[:, gs], ACT.Copy, scale=-1.0 / C).then_inc(s["xs_neg"], 1)
                        wait(act, s["xs_neg"], u, len(SQ_FILLS), n + 1)
                        if n == 0:
                            wait(act, s["px_var"], u, 1, 0)
                        wait(act, s["xs_sq"], u, len(SQ_FILLS), n)
                        wait(act, s["xT_done"], u, 8, SQ_FILLS[n - 1] + 1 if n else SQ_FILLS[-1] - 7)
                        for i, done in enumerate(("xs_sq", "xT_done")):
                            act.activation(x_sq[:, i, :], TX[f % 2][:, i * C:(i + 1) * C], ACT.Square,
                                           bias=x_neg[:, 2 * f + i:2 * f + i + 1],
                                           accum_out=v_a[:, 2 * f + i:2 * f + i + 1]).then_inc(s[done], 1)
                        continue
                    act.activation(xTh[u.x][:, 2 * f:2 * f + 2, :],
                                   TX[f % 2][:, :].rearrange("p (g c) -> p g c", c=C), ACT.Copy).then_inc(s["xT_done"], 1)

            def z_out(act, w, fills):
                for f in fills:
                    wait(act, s["z_ps"], w, 4, f + 1)
                    c, half = f // 2, f % 2
                    act.activation(zh[:, c, :, half * 64:half * 64 + 64], ZB[f % 2][:, :].rearrange("p (h n) -> p h n", n=64),
                                   ACT.Copy, scale=1.0 / WSC).then_inc(s["z_done"], 1)

            def u_out(act, u, f):
                wait(act, s["u_ps"], u, 4, f + 1)
                if f == 0:
                    wait(act, s["s_ps"], u, 2, -2)
                c, hh = f // 2, f % 2
                act.activation(u_s[u.two][:, c, hh * 4:hh * 4 + 4, :].rearrange("p h t -> p (h t)"),
                               US[1][:, :], ACT.Copy, scale=C ** -0.5 / WSC).then_inc(s["u_done"], 1)

            def slot(act, u, front, mid, back, end):
                v, w, z = u.before(), u.before(2), u.before(3)
                if front:
                    x_out(act, u, [0])
                if end:
                    wait(act, s["a_ps"], z, 1, 1)
                    act.activation(ag[:, :], MI[0][:, 0:C], ACT.Copy, scale=1.0 / WSC).then_inc(s["ag_done"], 1)
                if front:
                    wait(act, s["rT_ps"], u, 1, 1)
                    wait(act, s["rc_done"], u, 1, 0)
                    act.activation(rT[:, :], MI[1][:, 0:C], ACT.Copy, scale=1.0 / NPIX).then_inc(s["rT_done"], 1)
                    x_out(act, u, [1])
                if end:
                    wait(act, s["at_ps"], z, 1, 1)
                    act.activation(agT[:, :, :].rearrange("p c t -> p (c t)"), ZB[0][:, 0:C], ACT.Copy).then_inc(s["agT_done"], 1)
                if front:
                    x_out(act, u, [2, 3, 4])
                    wait(act, s["qs_ps"], u, 1, 1)
                    act.activation(qsT[:, :, :].rearrange("p h t -> p (h t)"), MI[1][:, :].bitcast(F16),
                                   ACT.Copy).then_inc(s["qsT_done"], 1)
                    u_out(act, u, 0)
                if back:
                    z_out(act, w, [0])
                if front:
                    x_out(act, u, [5])
                if end:
                    wait(act, s["nt_ps"], z, 1, 1)
                    act.activation(xnT[:, :, 0:P], MI[1][:, 0:C].rearrange("p (c t) -> p c t", t=P),
                                   ACT.Copy).then_inc(s["xnT_done"], 1)
                if back:
                    z_out(act, w, [1])
                if front:
                    u_out(act, u, 1)
                if end:
                    wait(act, s["h_ps"], z, 1, 1)
                    n = P + 1 if z.two == 0 else P
                    if z.two == 0:
                        b = z.j * HALVES + z.k // HALVES
                        if not (isinstance(b, int) and b == 0):
                            act.wait_ge(s["clsH_done"], b)
                    for m in range(CC):
                        act.activation(hT[z.two][:, m, 0:n], MI[0][:, m * 256:m * 256 + n], ACT.Tanh,
                                       bias=rnn_b[:, m:m + 1]).then_inc(s["hT_done"], 1)
                if front:
                    x_out(act, u, [6])
                if back:
                    z_out(act, w, [2])
                if front:
                    u_out(act, u, 2)
                if back:
                    z_out(act, w, [3])
                if mid:
                    wait(act, s["c_sub"], v, 1, 1)
                    act.activation(ex[:, :, :], lg[:, :, :], ACT.Exp).then_inc(s["ex_done"], 1)
                if front:
                    x_out(act, u, [7])
                    u_out(act, u, 3)
            over_slots(act, slot)

        @block.tensor
        def _(pe):
            mm = pe.matmul
            pe.wait_ge(s["consts_in"], 16 * NCONST)
            pe.wait_ge(s["avg_set"], 6)
            pe.wait_ge(s["prep_dve"], 4)
            for i, w in ((0, sq), (1, sv)):
                for c in range(CC):
                    last = mm(US[i][:, 0:C], avg[:, :], w[:, c, :], start=(c == 0), stop=(c == CC - 1))
                last.then_inc(s["prep_pe"], 1)
            for m in range(CC):
                for c in range(CC):
                    last = mm(MI[0][:, m:m + 1], raw_v[:, c, m * P:(m + 1) * P], lkv_b[:, c:c + 1],
                              start=(c == 0), stop=(c == CC - 1))
            last.then_inc(s["prep_pe"], 1)
            pe.wait_ge(s["prep_dve"], 6)
            for c in range(CC):
                last = mm(ZB[0][:, 0:C], bq_rep[:, c, :], raw_q[:, c, :], start=(c == 0), stop=(c == CC - 1))
            last.then_inc(s["prep_pe"], 1)
            pe.wait_ge(s["prep_dve"], 10)
            for c in range(CC):
                last = mm(ZB[1][:, 0:C], vb_rep[:, c, :], pj_s[:, c, :], start=(c == 0), stop=(c == CC - 1))
            last.then_inc(s["prep_pe"], 1)
            pe.wait_ge(s["cls_dve"], 4)
            for c in range(CC):
                last = pe.transpose(MI[1][:, c * B:(c + 1) * B], cxn[:, c * P:(c + 1) * P], ident[0:B, 0:B])
            last.then_inc(s["cls_pe"], 1)
            pe.wait_ge(s["w_ready_dve"], 1)
            pe.wait_ge(s["w_ready_act"], 1)

            def x_turn(pe, u, fills):
                for f in fills:
                    wait(pe, s["tx_free"], u, 8, f - 1)
                    for i in range(2):
                        g = 2 * f + i
                        for c in range(CC):
                            last = pe.transpose(TX[f % 2][:, i * C + c * P:i * C + (c + 1) * P],
                                                x_s[u.x][:, c, g * P:(g + 1) * P], ident[:, :])
                    last.then_inc(s["xT_ps"], 1)

            def weigh(pe, w, fills):
                for f in fills:
                    c, half = f // 2, f % 2
                    if f == 0:
                        wait(pe, s["pd_done"], w, 2, 2)
                        wait(pe, s["tx_free"], w, 8, 8)
                    elif f >= 2:
                        wait(pe, s["z_low"], w, 4, f - 1)
                    bank = ZB[f % 2][:, :].rearrange("p (h n) -> p h n", n=64)
                    for i in range(8):
                        g = half * 8 + i
                        o = bank[:, :, i * GP:(i + 1) * GP]
                        hi, lo = xTh[w.x][:, g, c * P:(c + 1) * P], xTl[w.x][:, g, c * P:(c + 1) * P]
                        mm(o, hi, pdh[:, g, :, :], start=True, stop=False)
                        mm(o, hi, pdl[:, g, :, :], start=False, stop=False)
                        last = mm(o, lo, pdh[:, g, :, :], start=False, stop=True)
                    last.then_inc(s["z_ps"], 1)

            def score(pe, v, quarter):
                f = quarter // 2
                if quarter == 0:
                    wait(pe, s["u_done"], v, 4, 4)
                    wait(pe, s["c_sub"], v, 1, 0)
                if quarter % 2 == 0:
                    wait(pe, s["s_masked"], v, 2, f)
                for i in range(4 * (quarter % 2), 4 * (quarter % 2) + 4):
                    g = f * 8 + i
                    for c in range(CC):
                        last = mm(US[0][:, i * 64:(i + 1) * 64], x_s[v.x][:, c, g * P:(g + 1) * P],
                                  u_s[v.two][:, c, :, g * GP:(g + 1) * GP], start=(c == 0), stop=(c == CC - 1))
                if quarter % 2:
                    last.then_inc(s["s_ps"], 1)

            def project(pe, u, f):
                if f == 0:
                    wait(pe, s["qsT_done"], u, 1, 1)
                wait(pe, s["u_done"], u, 4, f)
                c, hh = f // 2, f % 2
                for i in range(4):
                    h = hh * 4 + i
                    last = mm(US[1][:, i * P:(i + 1) * P], wk_st[:, h, c * P:(c + 1) * P], qsT[:, h, :],
                              start=True, stop=True)
                last.then_inc(s["u_ps"], 1)

            def values(pe, z):
                wait(pe, s["z_low"], z, 4, 4)
                for h in range(HEADS):
                    o = MI[0][:, h * D:(h + 1) * D]
                    for c in range(CC):
                        wh, wl = wvh[:, c, h * D:(h + 1) * D], wvl[:, c, h * D:(h + 1) * D]
                        mm(o, zh[:, c, h, :], wh, start=(c == 0), stop=False)
                        mm(o, zh[:, c, h, :], wl, start=False, stop=False)
                        last = mm(o, zl[:, c, h, :], wh, start=False, stop=(c == CC - 1))
                last.then_inc(s["a_ps"], 1)

            def recur(pe, z, m):
                n = P + 1 if z.two == 0 else P
                o = MI[0][:, m * 256:m * 256 + n]
                for c in range(CC):
                    mm(o, hh_s[:, c, m * P:(m + 1) * P], hT[z.two][:, c, 0:n], start=(c == 0), stop=False)
                if m == 0:
                    wait(pe, s["xnT_done"], z, 1, 1)
                for c in range(CC):
                    last = mm(o, ih_s[:, c, m * P:(m + 1) * P], xnT[:, c, 0:n], start=False, stop=(c == CC - 1))
                if m == CC - 1:
                    last.then_inc(s["h_ps"], 1)

            def slot(pe, u, front, mid, back, end):
                v, w, z = u.before(), u.before(2), u.before(3)
                if front:
                    wait_x(pe, u)
                    x_turn(pe, u, [0])
                if end:
                    values(pe, z)
                if front:
                    wait(pe, s["r_done"], u, 1, 1)
                    wait(pe, s["h2_done"], z, 1, 0)
                    for c in range(CC):
                        last = pe.transpose(MI[1][:, c * P:(c + 1) * P], r_s[u.two][:, c, :], ident[:, :])
                    last.then_inc(s["rT_ps"], 1)
                    x_turn(pe, u, [1])
                if mid:
                    score(pe, v, 0)
                if end:
                    wait(pe, s["ag_done"], z, 1, 1)
                    for c in range(CC):
                        last = pe.transpose(ZB[0][:, c * P:(c + 1) * P], ag[:, c * P:(c + 1) * P], ident[:, :])
                    last.then_inc(s["at_ps"], 1)
                if back:
                    wait(pe, s["p_done"], w, 1, 1)
                    pe.transpose(ZB[1][:, 0:P], pr[:, :, :].rearrange("p t n -> p (t n)"), ident[:, :]).then_inc(s["pt_ps"], 1)
                if mid:
                    score(pe, v, 1)
                if front:
                    x_turn(pe, u, [2])
                    for c in range(CC):
                        last = mm(MI[0][:, 0:C], r_s[u.two][:, c, :], wq_s[:, c, :], start=(c == 0), stop=(c == CC - 1))
                    last.then_inc(s["q_ps"], 1)
                if end:
                    wait(pe, s["agT_done"], z, 1, 1)
                    for c in range(CC):
                        last = mm(US[1][:, 0:C], agT[:, c, :], pj_s[:, c, :], start=(c == 0), stop=(c == CC - 1))
                    last.then_inc(s["pj_ps"], 1)
                if front:
                    x_turn(pe, u, [3])
                if mid:
                    score(pe, v, 2)
                if front:
                    x_turn(pe, u, [4])
                    wait(pe, s["q_split"], u, 3, 3)
                    wait(pe, s["rT_done"], u, 1, 1)
                    q16 = MI[1][:, :].bitcast(F16)
                    for h in range(HEADS):
                        last = pe.transpose(q16[:, h * P:(h + 1) * P], qs[:, h, :, :].rearrange("p a d -> p (a d)"),
                                            ident16[:, :])
                    last.then_inc(s["qs_ps"], 1)
                if mid:
                    score(pe, v, 3)
                if front:
                    if end:
                        wait(pe, s["h_done"], z, 1, 1)
                    project(pe, u, 0)
                if back:
                    weigh(pe, w, [0])
                if front:
                    x_turn(pe, u, [5])
                if end:
                    wait(pe, s["xn_done"], z, 1, 1)
                    if front:
                        wait(pe, s["qsT_done"], u, 1, 1)
                    for c in range(CC):
                        last = pe.transpose(MI[1][:, c * P:(c + 1) * P], xn[:, c * P:(c + 1) * P], ident[:, :])
                    last.then_inc(s["nt_ps"], 1)
                if back:
                    weigh(pe, w, [1])
                if front:
                    project(pe, u, 1)
                if end:
                    if front:
                        wait(pe, s["q_done"], u, 1, 1)
                    recur(pe, z, 0)
                if mid:
                    wait(pe, s["sc_done"], v, 1, 1)
                    pe.transpose(US[0][:, 0:P], sc2[:, :, :].rearrange("p g h -> p (g h)"), ident[:, :]).then_inc(s["c_ps"], 1)
                if end:
                    recur(pe, z, 1)
                if front:
                    x_turn(pe, u, [6])
                if back:
                    weigh(pe, w, [2])
                if front:
                    project(pe, u, 2)
                if back:
                    weigh(pe, w, [3])
                if end:
                    wait(pe, s["hT_done"], z, 2, 2)
                    for c in range(CC):
                        last = pe.transpose(MI[1][:, c * P:(c + 1) * P], hT[z.two][:, c, 0:P], ident[:, :])
                    last.then_inc(s["ht_ps"], 1)
                if front:
                    x_turn(pe, u, [7])
                if front:
                    project(pe, u, 3)
            over_slots(pe, slot)

        @block.vector
        def _(dve):
            n = [0]

            def chain(ins):
                n[0] += 1
                ins.then_inc(s["prep_dve"], 1)
                dve.wait_ge(s["prep_dve"], n[0])

            dve.wait_ge(s["consts_in"], 16 * NCONST)
            for c in range(CC):
                chain(dve.tensor_scalar(sq[:, c, :], raw_q[:, c, :], lq_w[:, c:c + 1], 1.0 / NPIX, ALU.mult, ALU.mult))
                chain(dve.tensor_scalar(sv[:, c, :], raw_v[:, c, :], lkv_w[:, c:c + 1], None, ALU.mult))
            for c in range(CC):
                chain(dve.tensor_scalar(bq_rep[:, c, :], ident[:, :], 0.0, lq_b[:, c:c + 1], ALU.mult, ALU.add))
            chain(dve.tensor_copy(ident16[:, :], ident[:, :]))
            dve.bn_stats(cst, cls_row[:, :]).then_inc(s["cls_dve"], 1)
            dve.wait_ge(s["cls_dve"], 1)
            dve.bn_aggr(cmv, cst).then_inc(s["cls_dve"], 1)
            dve.wait_ge(s["cls_dve"], 2)
            dve.tensor_scalar(cve, cmv[:, 1:2], EPS, None, ALU.add).then_inc(s["cls_dve"], 1)
            dve.wait_ge(s["cls_pool"], 1)
            dve.tensor_scalar(cxn, cls_row[:, :], cmv[:, 0:1], crs, ALU.subtract, ALU.mult).then_inc(s["cls_dve"], 1)
            dve.wait_ge(s["wk_in"], 64)
            chain(dve.tensor_tensor(stage_wk32, stage_wk, lkv_w_row[:, :].unsqueeze(1).to_broadcast([P, HEADS, C]), ALU.mult))
            dve.wait_ge(s["prep_act"], 3)
            for c in range(CC):
                chain(dve.tensor_scalar(vb_rep[:, c, :], ident[:, :], 0.0, vb_col[:, c:c + 1], ALU.mult, ALU.add))
            chain(dve.tensor_reduce(wk_sum, stage_wk32, X, ALU.add))
            chain(dve.tensor_scalar(wk_mean, wk_sum, -1.0 / C, None, ALU.mult))
            chain(dve.tensor_tensor(stage_wk32, stage_wk32, wk_mean.unsqueeze(2).to_broadcast([P, HEADS, C]), ALU.add))
            chain(dve.tensor_scalar(stage_wk, stage_wk32, WSC, None, ALU.mult))
            chain(dve.tensor_copy(wk_st[:, :, :], stage_wk))
            chain(dve.tensor_tensor(wk_st[64:128, :, :], stage_wk[64:128, :, :], wk_st[64:128, :, :], ALU.subtract))
            dve.wait_ge(s["prep_pe"], 5)
            for i, (w, dst) in enumerate(((sq, wq_s), (sv, cv32))):
                for c in range(CC):
                    chain(dve.tensor_tensor(dst[:, c, :], w[:, c, :], US[i][:, 0:C], ALU.subtract))
            chain(dve.tensor_scalar(wvh[:, :, :], cv32, WSC, None, ALU.mult))
            chain(dve.scalar_tensor_tensor(wvl[:, :, :], cv32, WSC, wvh[:, :, :], ALU.mult, ALU.subtract))
            chain(dve.tensor_copy(mask16[:, :], mask[:, :]))
            chain(dve.tensor_copy(qb_row[:, :], ZB[0][:, 0:C]))
            dve.tensor_tensor(cvec[:, :], ZB[1][:, 0:C], projb_row[:, :], ALU.add).then_inc(s["w_ready_dve"], 1)

            def x_low(dve, u, fills):
                for f in fills:
                    wait(dve, s["xT_done"], u, 8, f + 1)
                    ins = dve.tensor_tensor(xTl[u.x][:, 2 * f:2 * f + 2, :].rearrange("p g c -> p (g c)"), TX[f % 2][:, :],
                                            xTh[u.x][:, 2 * f:2 * f + 2, :].rearrange("p g c -> p (g c)"), ALU.subtract)
                    for i in range(0 if f in SQ_FILLS else 2):
                        ins = dve.bn_stats(st[:, 2 * f + i, :], TX[f % 2][:, i * C:(i + 1) * C])
                    ins.then_inc(s["tx_free"], 1)

            def z_out_low(dve, w, fills):
                for f in fills:
                    wait(dve, s["z_done"], w, 4, f + 1)
                    c, half = f // 2, f % 2
                    dve.scalar_tensor_tensor(zl[:, c, :, half * 64:half * 64 + 64], ZB[f % 2][:, :].rearrange("p (h n) -> p h n", n=64),
                                             1.0 / WSC, zh[:, c, :, half * 64:half * 64 + 64], ALU.mult,
                                             ALU.subtract).then_inc(s["z_low"], 1)

            def unmask(dve, v, f):
                wait(dve, s["s_ps"], v, 2, f + 1)
                dve.tensor_tensor(sm[:, :, :], US[0][:, :].rearrange("p (a t) -> p a t", t=GP),
                                  mask[:, :].unsqueeze(1).to_broadcast([P, G // 2 * HEADS, GP]), ALU.mult).then_inc(s["s_masked"], 1)
                wait(dve, s["s_masked"], v, 2, f + 1)
                dve.tensor_reduce(sc[:, f * 8:f * 8 + 8, :].rearrange("p g h -> p (g h)"), sm[:, :, :], X,
                                  ALU.add).then_inc(s["s_summed"], 1)

            def slot(dve, u, front, mid, back, end):
                v, w, z = u.before(), u.before(2), u.before(3)
                if back:
                    wait(dve, s["ex_done"], w, 1, 1)
                    dve.tensor_reduce(den[:, :], ex[:, :, :], X, ALU.add).then_inc(s["p_sum"], 1)
                    wait(dve, s["p_sum"], w, 1, 1)
                    dve.reciprocal(rden[:, :], den[:, :]).then_inc(s["p_rec"], 1)
                    wait(dve, s["p_rec"], w, 1, 1)
                    dve.tensor_tensor(pr[:, :, :], ex[:, :, :], rden[:, :].unsqueeze(2).to_broadcast([P, GP, NPIX]),
                                      ALU.mult).then_inc(s["p_done"], 1)
                if front:
                    x_low(dve, u, [0])
                    wait(dve, s["rT_done"], u, 1, 1)
                    dve.bn_stats(qst[:, :], rT[:, :]).then_inc(s["q_stat"], 1)
                    wait(dve, s["qve_done"], u, 1, 0)
                    wait(dve, s["q_stat"], u, 1, 1)
                    dve.memset(held[:, :], 0.0)
                    dve.bn_aggr(qmv[:, :], qst[:, :]).then_inc(s["q_var"], 1)
                    x_low(dve, u, [1])
                if back:
                    wait(dve, s["pt_ps"], w, 1, 1)
                    dve.scalar_tensor_tensor(pc[:, :, :], ZB[1][:, 0:P].rearrange("p (g h) -> p g h", h=HEADS), WSC,
                                             rs_px[w.two][:, :].unsqueeze(2).to_broadcast([P, G, HEADS]), ALU.mult,
                                             ALU.mult).then_inc(s["pc_done"], 1)
                    wait(dve, s["pc_done"], w, 1, 1)
                    wait(dve, s["pd_done"], w, 2, 0)
                    dve.tensor_copy(pch[:, :, :], pc[:, :, :]).then_inc(s["pc_split"], 1)
                    wait(dve, s["pc_split"], w, 2, 1)
                    dve.tensor_tensor(pcl[:, :, :], pc[:, :, :], pch[:, :, :], ALU.subtract).then_inc(s["pc_split"], 1)
                if mid:
                    unmask(dve, v, 0)
                if front:
                    x_low(dve, u, [2])
                    wait(dve, s["q_ps"], u, 1, 1)
                    wait(dve, s["q_rs_done"], u, 1, 1)
                    dve.scalar_tensor_tensor(q_s[:, :], MI[0][:, 0:C], q_rs[:, 0:1], qb_row[:, :], ALU.mult,
                                             ALU.add).then_inc(s["q_done"], 1)
                    wait(dve, s["q_done"], u, 1, 1)
                    qv = q_s[:, :].rearrange("p (h d) -> p h d", d=D)
                    dve.tensor_copy(qs[:, :, 0, :], qv).then_inc(s["q_split"], 1)
                    wait(dve, s["q_split"], u, 3, 1)
                    dve.tensor_tensor(qs[:, :, 1, :], qv, qs[:, :, 0, :], ALU.subtract).then_inc(s["q_split"], 1)
                    wait(dve, s["q_split"], u, 3, 2)
                    dve.tensor_copy(qs[:, :, 2:4, :], qs[:, :, 0:2, :]).then_inc(s["q_split"], 1)
                if end:
                    wait(dve, s["pj_ps"], z, 1, 1)
                    wait(dve, s["rc_done"], z, 1, 1)
                    wait(dve, s["h2_done"], z, 1, 0)
                    dve.tensor_tensor(h_s[:, :], US[1][:, 0:C], rc[z.x][:, :], ALU.add).then_inc(s["h_done"], 1)
                    wait(dve, s["h_done"], z, 1, 1)
                    dve.bn_stats(hst[:, :], h_s[:, :]).then_inc(s["h_stat"], 1)
                    wait(dve, s["hve_done"], z, 1, 0)
                    wait(dve, s["h_stat"], z, 1, 1)
                    dve.memset(held[:, :], 0.0)
                    dve.bn_aggr(hmv[:, :], hst[:, :]).then_inc(s["h_var"], 1)
                if front:
                    x_low(dve, u, [3])
                if end:
                    wait(dve, s["h_rs_done"], z, 1, 1)
                    dve.tensor_scalar(xn[:, :], h_s[:, :], hmv[:, 0:1], h_rs[:, 0:1], ALU.subtract,
                                      ALU.mult).then_inc(s["xn_done"], 1)
                if front:
                    x_low(dve, u, [4])
                if mid:
                    unmask(dve, v, 1)
                    wait(dve, s["s_summed"], v, 2, 2)
                    wait(dve, s["rs_px_done"], v, 1, 1)
                    dve.tensor_tensor(sc2[:, :, :], sc[:, :, :], rs_px[v.two][:, :].unsqueeze(2).to_broadcast([P, G, HEADS]),
                                      ALU.mult).then_inc(s["sc_done"], 1)
                if back:
                    z_out_low(dve, w, [0])
                if front:
                    x_low(dve, u, [5])
                if back:
                    z_out_low(dve, w, [1])
                if mid:
                    wait(dve, s["c_ps"], v, 1, 1)
                    cv = US[0][:, 0:P].rearrange("p (t n) -> p t n", n=NPIX)
                    dve.tensor_reduce(mx[:, :], cv, X, ALU.max).then_inc(s["c_max"], 1)
                    wait(dve, s["c_max"], v, 1, 1)
                    dve.tensor_tensor(lg[:, :, :], cv, mx[:, :].unsqueeze(2).to_broadcast([P, GP, NPIX]),
                                      ALU.subtract).then_inc(s["c_sub"], 1)
                if front:
                    x_low(dve, u, [6])
                if back:
                    z_out_low(dve, w, [2, 3])
                if end:
                    wait(dve, s["ht_ps"], z, 1, 1)
                    wait(dve, s["h2_out"], z, 16, 0)
                    dve.tensor_tensor(h2[:, :], MI[1][:, 0:C], h_s[:, :], ALU.add).then_inc(s["h2_done"], 1)
                if front:
                    x_low(dve, u, [7])
                    wait(dve, s["tx_free"], u, 8, 8)
                    NB = len(BN_FILLS)
                    for lo, hi in BN_FILLS:
                        gs = slice(lo * 2, hi * 2 + 2)
                        dve.tensor_tensor(v_b[:, gs], st[:, gs, 1], st[:, gs, 4], ALU.subtract).then_inc(s["px_ve_done"], 1)
                        dve.tensor_tensor(v_c[:, gs], st[:, gs, 2], st[:, gs, 5], ALU.add).then_inc(s["px_ve_done"], 1)
                    wait(dve, s["px_ve_done"], u, 2 * NB, 2 * NB)
                    for lo, hi in BN_FILLS:
                        gs = slice(lo * 2, hi * 2 + 2)
                        dve.scalar_tensor_tensor(v_d[:, gs], v_b[:, gs], C / 4.0, v_b[:, gs], ALU.mult, ALU.mult).then_inc(s["px_sq"], 1)
                    wait(dve, s["px_sq"], u, NB, NB)
                    for lo, hi in BN_FILLS:
                        gs = slice(lo * 2, hi * 2 + 2)
                        dve.tensor_tensor(v_a[:, gs], v_d[:, gs], v_c[:, gs], ALU.add).then_inc(s["px_ss"], 1)
                    wait(dve, s["px_ss"], u, NB, NB)
                    wait(dve, s["rs_px_done"], u, 1, 0)
                    dve.tensor_scalar(v_e[:, :], v_a[:, :], 1.0 / C, EPS, ALU.mult, ALU.add).then_inc(s["px_var"], 1)
            over_slots(dve, slot)

        tokens.close()
        stage_a.close()

        hc = [sb(f"hc{i}", [P, TPC, C]) for i in range(2)]
        tok = [sb(f"tok{i}", [P, TPC, C]) for i in range(2)]
        acc = [sb(f"acc{i}", [P, TPC, C]) for i in range(2)]
        th = [sb(f"th{i}", [P, CC, TPC * P], F16) for i in range(2)]
        tl = [sb(f"tl{i}", [P, CC, TPC * P], F16) for i in range(2)]
        g32 = [sb(f"g32_{i}", [P, CC, TPC * P]) for i in range(2)]
        gh = [sb(f"gh{i}", [P, CC, TPC * P], F16) for i in range(2)]
        gl = [sb(f"gl{i}", [P, CC, TPC * P], F16) for i in range(2)]
        w1h, w1l, w2h, w2l = [sb(n, [P, E, CC, C], F16) for n in ("w1h", "w1l", "w2h", "w2l")]
        WST = 4
        wst = [sb(f"wst{i}", [P, CC, C]) for i in range(WST)]
        est = sb("est", [P, TPC, 6])
        emv = sb("emv", [P, TPC, 2])
        eve = sb("eve", [P, TPC])
        ers = sb("ers", [P, TPC])
        comb = sb("comb", [P, TPC, E])
        combs = [sb(f"combs{i}", [P, TPC, E]) for i in range(2)]
        cT = sb("cT", [E, TPC * P])
        small = {n: sb(n, [P, TPC, E]) for n in "ls le pb eq1 cand1 oh1 p2 eq2 cand2 oh2 ct1 ct2".split()}
        tiny = {n: sb(n, [P, TPC]) for n in "lmx lsum lrec m1 i1 m2 i2 msum mcl mrec rw1 rw2".split()}
        rth = sb("rth", [P, CC, E], F16)
        rtl = sb("rtl", [P, CC, E], F16)
        rt32 = sb("rt32", [P, CC, E])
        b2_s = sb("b2_s", [E, C])
        iota8 = sb("iota8", [P, TPC, E])
        TT, LG, L1, Y = pbank[0:2], pbank[2], pbank[3:5], pbank[5:7]
        CL = pbank[7]
        names = """hc0_in hc1_in w_in ew_in w_hi w_lo rt_scaled rt_hi rt_lo cls_turned cls_h
            e_stat e_var e_ve e_rs tok_done base_done tt_ps th_done tl_done lg_ps le_done route comb_done ct_ps cT_done
            l1_ps g32_done gh_done gl_done y_ps y_done out0_done out1_done""".split()
        s = {n: sem("e_" + n) for n in names}
        w_in = [sem(f"e_wst{i}_in") for i in range(WST)]
        hc_in = [s["hc0_in"], s["hc1_in"]]
        out_done = [s["out0_done"], s["out1_done"]]
        ROUTE = 24
        YF = 2 * (E + 1)

        def over_chunks(eng, chunk):
            chunk(eng, Chunk(0, 0))
            half = (CHUNKS - 2) // 2
            with eng.Fori(0, half) as j:
                for k in (1, 2):
                    chunk(eng, Chunk(j, k))
            chunk(eng, Chunk(half, 1))
            chunk(eng, Chunk(half, 2, True))

        experts = ExitStack()
        block2 = experts.enter_context(nc.Block())

        @block2.sync
        def _(sp):
            chunks_in = h2_dram.rearrange("(n i) p c -> n p i c", i=TPC)

            def load_h(n, k):
                sp.dma_start(hc[k][:, :, :], chunks_in[n]).then_inc(hc_in[k], 16)
            load_h(0, 0)
            load_h(1, 1)
            sp.dma_start(rt32[:, :, :], routerT.rearrange("(c p) e -> p c e", p=P)).then_inc(s["ew_in"], 16)
            sp.dma_start(b2_s[:, :], b2).then_inc(s["ew_in"], 16)
            sp.dma_start(iota8[:, :, :], iota_in.rearrange("p (i e) -> p i e", e=E)).then_inc(s["ew_in"], 16)
            for n in range(2 * E):
                if n >= WST:
                    sp.wait_ge(s["w_lo"], n - WST + 1)
                w = w1 if n % 2 == 0 else w2
                sp.dma_start(wst[n % WST][:, :, :], w[n // 2].rearrange("(c p) n -> p c n", p=P)).then_inc(w_in[n % WST], 16)
            def chunk(sp, ch):
                if ch.last:
                    wait(sp, s["y_done"], ch, YF, E + 1)
                    sp.dma_start(out[:, 0, :], acc[ch.two][0:B, 0, :]).then_inc(out_done[0], 16)
                    return
                n = ch.j * 2 + ch.k
                imgs = [ch.j * (2 * TPC // HALVES) + (ch.k * (TPC // HALVES) + i) for i in range(TPC // HALVES)]
                if not isinstance(n, int):
                    imgs = [sp.snap(i, min_val=0, max_val=B - 1) for i in imgs]
                if not isinstance(n, int) or n + 2 < CHUNKS:
                    m = n + 2 if isinstance(n, int) else sp.snap(n + 2, min_val=0, max_val=CHUNKS - 1)
                    wait_all(sp, [(s["base_done"], ch, 1, 1)])
                    load_h(m, ch.two)
                wait_all(sp, [(s["y_done"], ch, YF, YF)])
                for i, img in enumerate(imgs):
                    sp.dma_start(out[img, 1:TOKS + 1, :].rearrange("(t p) c -> p t c", p=P),
                                 acc[ch.two][:, i * HALVES:(i + 1) * HALVES, :]).then_inc(out_done[ch.two], 16)
            chunk(sp, Chunk(0, 0))
            half = (CHUNKS - 2) // 2
            with sp.Fori(0, half - 1) as j:
                for k in (1, 2):
                    chunk(sp, Chunk(j, k))
            for k in (1, 2):
                chunk(sp, Chunk(half - 1, k))
            chunk(sp, Chunk(half, 1))
            chunk(sp, Chunk(half, 2, True))
            sp.wait_ge(out_done[0], 16 * (B // 2 + 1))
            sp.wait_ge(out_done[1], 16 * (B // 2))

        def wait_h(eng, ch):
            if ch.last:
                eng.wait_ge(s["cls_h"], 1)
            else:
                eng.wait_ge(hc_in[ch.two], ch.j * 16 + (ch.k // 2 + 1) * 16)

        @block2.gpsimd
        def _(pool):
            def prep(pool, ch):
                n, t = ch.rows, ch.tiles
                wait(pool, s["e_ve"], ch, 1, 1)
                pool.tensor_tensor(ers[0:n, 0:t], eve[0:n, 0:t], half_neg[0:n, 0:t], ALU.pow).then_inc(s["e_rs"], 1)
                wait(pool, s["tok_done"], ch, TPC, t)
                stored = (ch.j + ch.k // 2) * (16 * TPC // HALVES)
                if not isinstance(stored, int) or stored > 0:
                    pool.wait_ge(out_done[ch.two], stored)
                pool.tensor_tensor(acc[ch.two][0:n, 0:t, :], hc[ch.two][0:n, 0:t, :], tok[ch.two][0:n, 0:t, :],
                                   ALU.add).then_inc(s["base_done"], 1)
            def high(n):
                hi = w1h if n % 2 == 0 else w2h
                pool.wait_ge(w_in[n % WST], 16 * (n // WST + 1))
                pool.tensor_scalar(hi[:, n // 2, :, :], wst[n % WST][:, :, :], WSC, None, ALU.mult).then_inc(s["w_hi"], 1)

            prep(pool, Chunk(0, 0))
            for n in range(8):
                high(n)

            def chunk(pool, ch):
                if not ch.last:
                    prep(pool, ch.next())
                if isinstance(ch.j, int) and ch.j == 0 and ch.k == 0:
                    for n in range(8, 2 * E):
                        high(n)
            over_chunks(pool, chunk)

        @block2.scalar
        def _(act):
            def turned(act, ch):
                for c in range(CC):
                    wait(act, s["tt_ps"], ch, CC, c + 1)
                    act.activation(th[ch.two][:, c, 0:ch.cols], TT[c][:, 0:ch.cols], ACT.Copy).then_inc(s["th_done"], 1)

            def route_exp(act, ch):
                n, t = ch.rows, ch.tiles
                wait(act, s["route"], ch, ROUTE, 2)
                act.activation(small["le"][0:n, 0:t, :], small["ls"][0:n, 0:t, :], ACT.Exp,
                               scale=1.0 / WSC).then_inc(s["le_done"], 1)

            def gates_turned(act, ch):
                wait(act, s["ct_ps"], ch, 1, 1)
                act.activation(cT[:, 0:ch.cols], TT[0][0:E, 0:ch.cols], ACT.Copy).then_inc(s["cT_done"], 1)

            def gelus(act, ch, e):
                for m in range(CC):
                    wait(act, s["l1_ps"], ch, 2 * E, 2 * e + m + 1)
                    for dst, done in ((g32, "g32_done"), (gh, "gh_done")):
                        act.activation(dst[e % 2][:, m, 0:ch.cols], L1[m][:, 0:ch.cols], ACT.Gelu,
                                       bias=b1_s[:, e, m:m + 1], scale=1.0 / WSC).then_inc(s[done], 1)

            act.wait_ge(s["rt_lo"], 1)
            turned(act, Chunk(0, 0))
            route_exp(act, Chunk(0, 0))

            def chunk(act, ch):
                zero = isinstance(ch.j, int) and ch.j == 0 and ch.k == 0
                for e in range(E):
                    if not ch.last:
                        if e == 4:
                            turned(act, ch.next())
                        if e == 7:
                            route_exp(act, ch.next())
                    gelus(act, ch, e)
                    if zero and e == 0:
                        gates_turned(act, ch)
                if not ch.last:
                    gates_turned(act, ch.next())
            over_chunks(act, chunk)

        @block2.tensor
        def _(pe):
            mm = pe.matmul

            def turn(pe, ch):
                n = ch.rows
                wait(pe, s["cT_done"], ch, 1, 0)
                wait(pe, s["tl_done"], ch, CC, 0)
                for c in range(CC):
                    for i in range(ch.tiles):
                        wait(pe, s["tok_done"], ch, TPC, i + 1)
                        last = pe.transpose(TT[c][:, i * n:(i + 1) * n], tok[ch.two][0:n, i, c * P:(c + 1) * P], ident[0:n, 0:n])
                    last.then_inc(s["tt_ps"], 1)

            def logits(pe, ch):
                n = ch.rows
                wait(pe, s["th_done"], ch, CC, CC)
                wait(pe, s["tl_done"], ch, CC, CC)
                for i in range(ch.tiles):
                    o = LG[0:n, i * E:(i + 1) * E]
                    for c in range(CC):
                        for a, t in enumerate((th, tl)):
                            for b, r in enumerate((rth, rtl)):
                                last = mm(o, t[ch.two][:, c, i * n:(i + 1) * n], r[:, c, :], start=(c + a + b == 0),
                                          stop=(c + a + b == CC + 1))
                last.then_inc(s["lg_ps"], 1)

            def gates(pe, ch):
                n = ch.rows
                wait(pe, s["comb_done"], ch, 1, 1)
                for i in range(ch.tiles):
                    last = pe.transpose(TT[0][0:E, i * n:(i + 1) * n], comb[0:n, i, :], ident[0:n, 0:n])
                last.then_inc(s["ct_ps"], 1)

            def first(pe, ch, e):
                for m in range(CC):
                    wait(pe, s["gh_done"], ch, 2 * E, 2 * e + m - 1)
                    o = L1[m][:, 0:ch.cols]
                    for c in range(CC):
                        wh, wl = w1h[:, e, c, m * P:(m + 1) * P], w1l[:, e, c, m * P:(m + 1) * P]
                        xh, xl = th[ch.two][:, c, 0:ch.cols], tl[ch.two][:, c, 0:ch.cols]
                        mm(o, wh, xh, start=(c == 0), stop=False)
                        mm(o, wh, xl, start=False, stop=False)
                        last = mm(o, wl, xh, start=False, stop=(c == CC - 1))
                    last.then_inc(s["l1_ps"], 1)

            def out_fill(pe, ch, step, p):
                f = step * ch.fills + p
                wait(pe, s["y_done"], ch, YF, f - 1)
                return Y[f % 2]

            def bias2(pe, ch):
                n = ch.rows
                wait(pe, s["cT_done"], ch, 1, 1)
                for p in range(ch.fills):
                    bank = out_fill(pe, ch, 0, p)
                    for i in range(2 * p, min(2 * p + 2, ch.tiles)):
                        last = mm(bank[0:n, (i % 2) * C:(i % 2 + 1) * C], cT[:, i * n:(i + 1) * n], b2_s[:, :], start=True, stop=True)
                    last.then_inc(s["y_ps"], 1)

            def second(pe, ch, e):
                n = ch.rows
                wait(pe, s["gh_done"], ch, 2 * E, 2 * e + 2)
                wait(pe, s["gl_done"], ch, 2 * E, 2 * e + 2)
                for p in range(ch.fills):
                    bank = out_fill(pe, ch, e + 1, p)
                    for i in range(2 * p, min(2 * p + 2, ch.tiles)):
                        o = bank[0:n, (i % 2) * C:(i % 2 + 1) * C]
                        for c in range(CC):
                            hi, lo = gh[e % 2][:, c, i * n:(i + 1) * n], gl[e % 2][:, c, i * n:(i + 1) * n]
                            mm(o, hi, w2h[:, e, c, :], start=(c == 0), stop=False)
                            mm(o, hi, w2l[:, e, c, :], start=False, stop=False)
                            last = mm(o, lo, w2h[:, e, c, :], start=False, stop=(c == CC - 1))
                    last.then_inc(s["y_ps"], 1)

            for c in range(CC):
                last = pe.transpose(CL[0:B, c * P:(c + 1) * P], clsH[:, c, :], ident[:, :])
            last.then_inc(s["cls_turned"], 1)
            turn(pe, Chunk(0, 0))
            pe.wait_ge(s["rt_lo"], 1)
            logits(pe, Chunk(0, 0))

            def chunk(pe, ch):
                zero = isinstance(ch.j, int) and ch.j == 0 and ch.k == 0
                for e in range(E):
                    if zero:
                        pe.wait_ge(s["w_lo"], 2 * e + 2)
                    first(pe, ch, e)
                    if e == 0:
                        if zero:
                            gates(pe, ch)
                        pe.wait_ge(s["ew_in"], 48)
                        bias2(pe, ch)
                    else:
                        second(pe, ch, e - 1)
                    if not ch.last:
                        if e == 3:
                            turn(pe, ch.next())
                        if e == 5:
                            logits(pe, ch.next())
                        if e == 7:
                            gates(pe, ch.next())
                second(pe, ch, E - 1)
            over_chunks(pe, chunk)

        @block2.vector
        def _(dve):
            def stats(dve, ch):
                n = ch.rows
                wait_h(dve, ch)
                for i in range(ch.tiles):
                    dve.bn_stats(est[0:n, i, :], hc[ch.two][0:n, i, :]).then_inc(s["e_stat"], 1)
                wait(dve, s["e_stat"], ch, TPC, ch.tiles)
                dve.memset(held[:, :], 0.0)
                for i in range(ch.tiles):
                    dve.bn_aggr(emv[0:n, i, :], est[0:n, i, :]).then_inc(s["e_var"], 1)
                wait(dve, s["e_var"], ch, TPC, ch.tiles)
                dve.tensor_scalar(eve[0:n, 0:ch.tiles], emv[0:n, 0:ch.tiles, 1], EPS, None, ALU.add).then_inc(s["e_ve"], 1)

            def normal(dve, ch):
                n = ch.rows
                wait(dve, s["e_rs"], ch, 1, 1)
                for i in range(ch.tiles):
                    dve.tensor_scalar(tok[ch.two][0:n, i, :], hc[ch.two][0:n, i, :], emv[0:n, i, 0:1], ers[0:n, i:i + 1],
                                      ALU.subtract, ALU.mult).then_inc(s["tok_done"], 1)

            def low(dve, ch):
                for c in range(CC):
                    wait(dve, s["th_done"], ch, CC, c + 1)
                    dve.tensor_tensor(tl[ch.two][:, c, 0:ch.cols], TT[c][:, 0:ch.cols], th[ch.two][:, c, 0:ch.cols],
                                      ALU.subtract).then_inc(s["tl_done"], 1)

            def route(dve, ch, part):
                n, t = ch.rows, ch.tiles
                S = {k: a[0:n, 0:t, :] for k, a in small.items()}
                T = {k: a[0:n, 0:t] for k, a in tiny.items()}
                over = lambda a: a.unsqueeze(2).to_broadcast([n, t, E])
                io = iota8[0:n, 0:t, :]
                count = [2 * part]

                def step(ins):
                    count[0] += 1
                    ins.then_inc(s["route"], 1)
                    wait(dve, s["route"], ch, ROUTE, count[0])

                lg = LG[0:n, 0:t * E].rearrange("p (t e) -> p t e", e=E)
                wait(dve, s["lg_ps"], ch, 1, 1)
                if part == 0:
                    step(dve.tensor_reduce(T["lmx"], lg, X, ALU.max))
                    step(dve.tensor_tensor(S["ls"], lg, over(T["lmx"]), ALU.subtract))
                    return
                wait(dve, s["le_done"], ch, 1, 1)
                step(dve.tensor_reduce(T["lsum"], S["le"], X, ALU.add))
                step(dve.reciprocal(T["lrec"], T["lsum"]))
                step(dve.tensor_tensor(S["pb"], S["le"], over(T["lrec"]), ALU.mult))
                for prob, m, eq, cand, i, oh in (("pb", "m1", "eq1", "cand1", "i1", "oh1"), ("p2", "m2", "eq2", "cand2", "i2", "oh2")):
                    step(dve.tensor_reduce(T[m], S[prob], X, ALU.max))
                    step(dve.tensor_tensor(S[eq], S[prob], over(T[m]), ALU.is_equal))
                    step(dve.tensor_tensor(S[cand], S[eq], io, ALU.mult))
                    step(dve.tensor_reduce(T[i], S[cand], X, ALU.min))
                    step(dve.tensor_tensor(S[oh], io, over(T[i]), ALU.is_equal))
                    if prob == "pb":
                        step(dve.scalar_tensor_tensor(S["p2"], S["oh1"], -4.0, S["pb"], ALU.mult, ALU.add))
                step(dve.tensor_tensor(T["msum"], T["m1"], T["m2"], ALU.add))
                step(dve.tensor_scalar(T["mcl"], T["msum"], 1e-12, None, ALU.max))
                step(dve.reciprocal(T["mrec"], T["mcl"]))
                step(dve.tensor_tensor(T["rw1"], T["m1"], T["mrec"], ALU.mult))
                step(dve.tensor_tensor(T["rw2"], T["m2"], T["mrec"], ALU.mult))
                step(dve.tensor_tensor(S["ct1"], S["oh1"], over(T["rw1"]), ALU.mult))
                step(dve.tensor_tensor(S["ct2"], S["oh2"], over(T["rw2"]), ALU.mult))
                wait(dve, s["ct_ps"], ch, 1, 0)
                step(dve.tensor_tensor(comb[0:n, 0:t, :], S["ct1"], S["ct2"], ALU.add))
                assert count[0] == ROUTE
                dve.tensor_scalar(combs[ch.two][0:n, 0:t, :], comb[0:n, 0:t, :], 1.0 / WSC, None, ALU.mult)\
                   .then_inc(s["comb_done"], 1)

            def gelu_low(dve, ch, e):
                for m in range(CC):
                    wait(dve, s["g32_done"], ch, 2 * E, 2 * e + m + 1)
                    wait(dve, s["gh_done"], ch, 2 * E, 2 * e + m + 1)
                    dve.tensor_tensor(gl[e % 2][:, m, 0:ch.cols], g32[e % 2][:, m, 0:ch.cols], gh[e % 2][:, m, 0:ch.cols],
                                      ALU.subtract).then_inc(s["gl_done"], 1)

            def add_out(dve, ch, step):
                n = ch.rows
                a = acc[ch.two]
                for p in range(ch.fills):
                    f = step * ch.fills + p
                    wait(dve, s["y_ps"], ch, YF, f + 1)
                    if step == 0:
                        wait(dve, s["base_done"], ch, 1, 1)
                        k = min(2, ch.tiles)
                        ins = dve.tensor_tensor(a[0:n, 2 * p:2 * p + k, :].rearrange("p t c -> p (t c)"), Y[f % 2][0:n, 0:k * C],
                                                a[0:n, 2 * p:2 * p + k, :].rearrange("p t c -> p (t c)"), ALU.add)
                    else:
                        e = step - 1
                        wait(dve, s["comb_done"], ch, 1, 1)
                        wait(dve, s["y_done"], ch, YF, f - ch.fills + 1)
                        for i in range(2 * p, min(2 * p + 2, ch.tiles)):
                            ins = dve.scalar_tensor_tensor(a[0:n, i, :], Y[f % 2][0:n, (i % 2) * C:(i % 2 + 1) * C],
                                                           combs[ch.two][0:n, i, e:e + 1], a[0:n, i, :], ALU.mult, ALU.add)
                    ins.then_inc(s["y_done"], 1)

            def prep(dve, ch):
                stats(dve, ch)
                normal(dve, ch)

            prep(dve, Chunk(0, 0))
            dve.wait_ge(s["ew_in"], 48)
            dve.tensor_scalar(rt32[:, :, :], rt32[:, :, :], WSC, None, ALU.mult).then_inc(s["rt_scaled"], 1)
            dve.wait_ge(s["rt_scaled"], 1)
            dve.tensor_copy(rth[:, :, :], rt32[:, :, :]).then_inc(s["rt_hi"], 1)
            dve.wait_ge(s["rt_hi"], 1)
            dve.tensor_tensor(rtl[:, :, :], rt32[:, :, :], rth[:, :, :], ALU.subtract).then_inc(s["rt_lo"], 1)
            def split(n):
                e = n // 2
                hi, lo = (w1h, w1l) if n % 2 == 0 else (w2h, w2l)
                dve.wait_ge(s["w_hi"], n + 1)
                dve.scalar_tensor_tensor(lo[:, e, :, :], wst[n % WST][:, :, :], WSC, hi[:, e, :, :], ALU.mult,
                                         ALU.subtract).then_inc(s["w_lo"], 1)

            low(dve, Chunk(0, 0))
            split(0)
            split(1)
            route(dve, Chunk(0, 0), 0)
            route(dve, Chunk(0, 0), 1)

            def chunk(dve, ch):
                zero = isinstance(ch.j, int) and ch.j == 0 and ch.k == 0
                for e in range(E):
                    if zero and e < E - 1:
                        split(2 * e + 2)
                        split(2 * e + 3)
                    gelu_low(dve, ch, e)
                    add_out(dve, ch, e)
                    if not ch.last:
                        if e == 1:
                            if ch.next().last:
                                dve.wait_ge(s["cls_turned"], 1)
                                wait(dve, s["base_done"], ch, 1, 0)
                                dve.tensor_tensor(hc[0][0:B, 0, :], CL[0:B, 0:C], cls_row[:, :], ALU.add).then_inc(s["cls_h"], 1)
                            stats(dve, ch.next())
                        if e == 2:
                            normal(dve, ch.next())
                        if e == 4:
                            low(dve, ch.next())
                        if e == 5:
                            route(dve, ch.next(), 0)
                        if e == 6:
                            route(dve, ch.next(), 1)
                add_out(dve, ch, E)
            over_chunks(dve, chunk)
        experts.close()


def kernel(x, cls_tok, L0_tok_ln_q_w, L0_tok_ln_q_b, L0_tok_Wq, L0_tok_ln_kv_w, L0_tok_ln_kv_b, L0_tok_Wkv,
           L0_tok_proj_w, L0_tok_proj_b, L0_attn_W_ih, L0_attn_W_hh, L0_attn_b_ih, L0_attn_b_hh,
           L0_ffn_router_w, L0_ffn_w1, L0_ffn_b1, L0_ffn_w2, L0_ffn_b2):
    import numpy as np
    import concourse.bacc as bacc
    from concourse import mybir as mb
    from concourse.bass_utils import run_bass_kernel_spmd

    h = IMG // STRIDE
    xg = np.asarray(x).reshape(B, C // P, P, h, STRIDE, h, STRIDE).transpose(0, 3, 2, 1, 5, 4, 6)
    xg = xg.reshape(B, HALVES, h // HALVES, P, C // P, h, NPIX).transpose(0, 1, 3, 4, 2, 5, 6).reshape(UNITS, P, C // P, PIX)
    pix = np.arange(P)

    def col(a):
        return np.asarray(a).reshape(C // P, P).T

    arrays = {
        "xg": xg, "cls_tok": np.asarray(cls_tok).reshape(C),
        "ln_q_w": col(L0_tok_ln_q_w), "ln_q_b": col(L0_tok_ln_q_b), "wqT": np.asarray(L0_tok_Wq).T,
        "ln_kv_w": L0_tok_ln_kv_w, "ln_kv_w_col": col(L0_tok_ln_kv_w), "ln_kv_b": col(L0_tok_ln_kv_b),
        "wk": np.asarray(L0_tok_Wkv)[:C], "wvT": np.asarray(L0_tok_Wkv)[C:].T,
        "projT": np.asarray(L0_tok_proj_w).T, "proj_b": L0_tok_proj_b,
        "wihT": np.asarray(L0_attn_W_ih).T, "whhT": np.asarray(L0_attn_W_hh).T,
        "b_ih": col(L0_attn_b_ih), "b_hh": col(L0_attn_b_hh),
        "routerT": np.asarray(L0_ffn_router_w).T, "w1": L0_ffn_w1,
        "b1": np.asarray(L0_ffn_b1).reshape(E * (C // P), P).T, "w2": L0_ffn_w2, "b2": L0_ffn_b2,
        "ident_in": np.eye(P, dtype=np.float32),
        "mask_in": (pix[:, None] // NPIX == np.arange(GP)[None, :]).astype(np.float32),
        "iota_in": np.tile(np.arange(E, dtype=np.float32) - E, (P, TPC)),
    }
    arrays = {k: np.ascontiguousarray(v) for k, v in arrays.items()}
    nc = bacc.Bacc("TRN2", target_bir_lowering=False, num_devices=1)
    args = [nc.dram_tensor(k, v.shape, mb.dt.from_np(v.dtype), kind="ExternalInput").ap() for k, v in arrays.items()]
    out = nc.dram_tensor("tower_out", (B, TOKS + 1, C), mb.dt.from_np(np.dtype("float32")), kind="ExternalOutput").ap()
    vit_tower(nc, *args, out)
    r = run_bass_kernel_spmd(nc, [arrays], core_ids=[0])
    return r.results[0]["tower_out"]
```
